# Optimizing a Trainium2 kernel written in Bass

```python
import numpy as np
import jax
import jax.numpy as jnp

def _softmax(x, axis=-1):
    return jax.nn.softmax(x, axis=axis)

def _gelu(x):
    return jax.nn.gelu(x, approximate=True)

def _silu(x):
    return jax.nn.silu(x)

def _sigmoid(x):
    return jax.nn.sigmoid(x)

def _layernorm(x, axis=-1, eps=1e-05):
    m = jnp.mean(x, axis=axis, keepdims=True)
    v = jnp.var(x, axis=axis, keepdims=True)
    return (x - m) / jnp.sqrt(v + eps)

def _scatter_add(tgt, idx, src, axis=0):
    return tgt.at[idx].add(src)

def _segment_sum(src, seg, n):
    return jax.ops.segment_sum(src, seg, n)
kernel_name = 'mk_adaln_d2_jaxref_r8_f68f57'

def setup_inputs(seed: int=0):
    np.random.seed(seed)
    _w = jnp.asarray

    def _L0_attn_setup():
        import jax, jax.numpy as jnp
        import numpy as np
        HIDDEN = 128
        NUM_HEADS = 16
        HEAD_DIM = 64
        NUM_KV_HEADS = 4

        def _xavier(key, out_dim, in_dim):
            limit = jnp.sqrt(6.0 / (in_dim + out_dim)).astype(jnp.float32)
            return jax.random.uniform(key, (out_dim, in_dim), jnp.float32, -limit, limit)
        key = jax.random.key(seed)
        kx, kq, kk, kv, ko = jax.random.split(key, 5)
        return {'hidden_states': jax.random.normal(kx, (2, 256, HIDDEN), jnp.float32), 'Wq': _xavier(kq, NUM_HEADS * HEAD_DIM, HIDDEN), 'Wk': _xavier(kk, NUM_KV_HEADS * HEAD_DIM, HIDDEN), 'Wv': _xavier(kv, NUM_KV_HEADS * HEAD_DIM, HIDDEN), 'Wo': _xavier(ko, HIDDEN, NUM_HEADS * HEAD_DIM)}
    _L0_attn_in = _L0_attn_setup()

    def _L0_ffn_setup():
        import jax, jax.numpy as jnp
        import numpy as np
        E = 32
        K = 4
        H = 128
        I = 96
        ROUTED_SCALING_FACTOR = 1.0
        key = jax.random.key(seed)
        k0, k1, k2, k3, k4, k5 = jax.random.split(key, 6)
        return {'hidden_states': jax.random.normal(k0, (1, 256, H), jnp.float32), 'gate_w': jax.random.normal(k1, (E, H), jnp.float32) * 0.02, 'w1': jax.random.normal(k2, (E, H, I), jnp.float32) * 0.02, 'w3': jax.random.normal(k3, (E, H, I), jnp.float32) * 0.02, 'w2': jax.random.normal(k4, (E, I, H), jnp.float32) * 0.02, 'e_bias': jax.random.normal(k5, (E,), jnp.float32) * 0.02}
    _L0_ffn_in = _L0_ffn_setup()
    _L0_c = _w((lambda *s: np.random.randn(*s).astype(np.float32) * 0.05)(2, 128))
    _L0_wmod = _w((lambda *s: np.random.randn(*s).astype(np.float32) * 0.05)(128, 6 * 128) * 128 ** (-0.5))

    def _L1_attn_setup():
        import jax, jax.numpy as jnp
        import numpy as np
        EPS = 1e-06
        N_HEADS = 16

        def _heads(t, B, N, H, Dk):
            return t.reshape(B, N, H, Dk).transpose(0, 2, 1, 3)
        key = jax.random.key(seed)
        ks = jax.random.split(key, 5)
        B, N, D = (64, 64, 128)
        x = jax.random.normal(ks[0], (B, N, D), dtype=jnp.float32)
        s = 0.02
        W_q = jax.random.normal(ks[1], (D, D), dtype=jnp.float32) * s
        W_k = jax.random.normal(ks[2], (D, D), dtype=jnp.float32) * s
        W_v = jax.random.normal(ks[3], (D, D), dtype=jnp.float32) * s
        W_o = jax.random.normal(ks[4], (D, D), dtype=jnp.float32) * s
        z = jnp.zeros((D,), dtype=jnp.float32)
        return {'x': x, 'W_q': W_q, 'b_q': z, 'W_k': W_k, 'b_k': z, 'W_v': W_v, 'b_v': z, 'W_o': W_o, 'b_o': z}
    _L1_attn_in = _L1_attn_setup()

    def _L1_ffn_setup():
        import jax, jax.numpy as jnp
        import numpy as np
        DIM = 128
        NQ = 16
        NKV = 4
        HD = DIM // NQ
        HID = 256
        E = 8
        B, S = (1, 128)
        EPS = 1e-06

        def rmsnorm(x, w):
            ms = jnp.mean(x * x, axis=-1, keepdims=True)
            return w * (x * jax.lax.rsqrt(ms + EPS))

        def rope_tables(seq_len, head_dim):
            inv_freq = 1.0 / 10000.0 ** (jnp.arange(0, head_dim, 2, dtype=jnp.float32) / head_dim)
            t = jnp.arange(seq_len, dtype=jnp.float32)
            freqs = jnp.einsum('i,j->ij', t, inv_freq)
            return (jnp.cos(freqs), jnp.sin(freqs))

        def apply_rope(x, cos, sin):
            c = cos[None, :, None, :]
            s = sin[None, :, None, :]
            half = x.shape[-1] // 2
            x1, x2 = (x[..., :half], x[..., half:])
            return jnp.concatenate([x1 * c - x2 * s, x1 * s + x2 * c], axis=-1)

        def _forward(x, ln1_w, ln2_w, Wq, bq, Wk, bk, Wv, bv, qn_w, kn_w, Wg, bg, Wo, bo, Wr, br, W1, b1, W2, b2):
            batch, seq, _ = x.shape
            cos, sin = rope_tables(seq, HD)
            h = rmsnorm(x, ln1_w)
            q = (h @ Wq + bq).reshape(batch, seq, NQ, HD)
            k = (h @ Wk + bk).reshape(batch, seq, NKV, HD)
            v = (h @ Wv + bv).reshape(batch, seq, NKV, HD)
            q = rmsnorm(apply_rope(q, cos, sin), qn_w)
            k = rmsnorm(apply_rope(k, cos, sin), kn_w)
            rep = NQ // NKV
            k = jnp.repeat(k, rep, axis=2)
            v = jnp.repeat(v, rep, axis=2)
            scores = jnp.einsum('bthd,bshd->bhts', q, k) / np.sqrt(HD)
            causal = jnp.tril(jnp.ones((seq, seq), dtype=bool))
            scores = jnp.where(causal[None, None], scores, -jnp.inf)
            attn = jax.nn.softmax(scores, axis=-1)
            out = jnp.einsum('bhts,bshd->bthd', attn, v)
            gate = jax.nn.sigmoid(out @ Wg + bg)
            out = (out * gate).reshape(batch, seq, DIM)
            x = x + out @ Wo + bo
            h2 = rmsnorm(x, ln2_w)
            logits = h2 @ Wr + br
            top1 = jnp.argmax(logits, axis=-1).reshape(-1)
            xt = h2.reshape(-1, DIM)
            u = jnp.einsum('td,edf->tef', xt, W1) + b1
            u1, u2 = (u[..., :HID], u[..., HID:])
            act = u1 * jax.nn.sigmoid(u2)
            y_all = jnp.einsum('teh,ehd->ted', act, W2) + b2
            y = jnp.take_along_axis(y_all, top1[:, None, None], axis=1)[:, 0, :]
            return x + y.reshape(batch, seq, DIM)
        key = jax.random.key(seed)
        ks = jax.random.split(key, 20)
        sc = lambda fan_in: 1.0 / np.sqrt(fan_in)
        d = {}
        d['x'] = jax.random.normal(ks[0], (B, S, DIM), dtype=jnp.float32)
        d['ln1_w'] = jnp.ones((DIM,), jnp.float32)
        d['ln2_w'] = jnp.ones((DIM,), jnp.float32)
        d['Wq'] = jax.random.normal(ks[1], (DIM, DIM), jnp.float32) * sc(DIM)
        d['bq'] = jnp.zeros((DIM,), jnp.float32)
        d['Wk'] = jax.random.normal(ks[2], (DIM, HD * NKV), jnp.float32) * sc(DIM)
        d['bk'] = jnp.zeros((HD * NKV,), jnp.float32)
        d['Wv'] = jax.random.normal(ks[3], (DIM, HD * NKV), jnp.float32) * sc(DIM)
        d['bv'] = jnp.zeros((HD * NKV,), jnp.float32)
        d['qn_w'] = jnp.ones((HD,), jnp.float32)
        d['kn_w'] = jnp.ones((HD,), jnp.float32)
        d['Wg'] = jax.random.normal(ks[4], (HD, HD), jnp.float32) * sc(HD)
        d['bg'] = jnp.zeros((HD,), jnp.float32)
        d['Wo'] = jax.random.normal(ks[5], (DIM, DIM), jnp.float32) * sc(DIM)
        d['bo'] = jnp.zeros((DIM,), jnp.float32)
        d['Wr'] = jax.random.normal(ks[6], (DIM, E), jnp.float32) * sc(DIM)
        d['br'] = jnp.zeros((E,), jnp.float32)
        d['W1'] = jax.random.normal(ks[7], (E, DIM, 2 * HID), jnp.float32) * sc(DIM)
        d['b1'] = jnp.zeros((E, 2 * HID), jnp.float32)
        d['W2'] = jax.random.normal(ks[8], (E, HID, DIM), jnp.float32) * sc(HID)
        d['b2'] = jnp.zeros((E, DIM), jnp.float32)
        return d
    _L1_ffn_in = _L1_ffn_setup()
    _L1_c = _w((lambda *s: np.random.randn(*s).astype(np.float32) * 0.05)(2, 128))
    _L1_wmod = _w((lambda *s: np.random.randn(*s).astype(np.float32) * 0.05)(128, 6 * 128) * 128 ** (-0.5))
    _d = {'L0_attn_hidden_states': _L0_attn_in['hidden_states'], 'L0_attn_Wq': _L0_attn_in['Wq'], 'L0_attn_Wk': _L0_attn_in['Wk'], 'L0_attn_Wv': _L0_attn_in['Wv'], 'L0_attn_Wo': _L0_attn_in['Wo'], 'L0_ffn_gate_w': _L0_ffn_in['gate_w'], 'L0_ffn_w1': _L0_ffn_in['w1'], 'L0_ffn_w3': _L0_ffn_in['w3'], 'L0_ffn_w2': _L0_ffn_in['w2'], 'L0_ffn_e_bias': _L0_ffn_in['e_bias'], 'L0_c': _L0_c, 'L0_wmod': _L0_wmod, 'L1_attn_W_q': _L1_attn_in['W_q'], 'L1_attn_b_q': _L1_attn_in['b_q'], 'L1_attn_W_k': _L1_attn_in['W_k'], 'L1_attn_b_k': _L1_attn_in['b_k'], 'L1_attn_W_v': _L1_attn_in['W_v'], 'L1_attn_b_v': _L1_attn_in['b_v'], 'L1_attn_W_o': _L1_attn_in['W_o'], 'L1_attn_b_o': _L1_attn_in['b_o'], 'L1_ffn_ln1_w': _L1_ffn_in['ln1_w'], 'L1_ffn_ln2_w': _L1_ffn_in['ln2_w'], 'L1_ffn_Wq': _L1_ffn_in['Wq'], 'L1_ffn_bq': _L1_ffn_in['bq'], 'L1_ffn_Wk': _L1_ffn_in['Wk'], 'L1_ffn_bk': _L1_ffn_in['bk'], 'L1_ffn_Wv': _L1_ffn_in['Wv'], 'L1_ffn_bv': _L1_ffn_in['bv'], 'L1_ffn_qn_w': _L1_ffn_in['qn_w'], 'L1_ffn_kn_w': _L1_ffn_in['kn_w'], 'L1_ffn_Wg': _L1_ffn_in['Wg'], 'L1_ffn_bg': _L1_ffn_in['bg'], 'L1_ffn_Wo': _L1_ffn_in['Wo'], 'L1_ffn_bo': _L1_ffn_in['bo'], 'L1_ffn_Wr': _L1_ffn_in['Wr'], 'L1_ffn_br': _L1_ffn_in['br'], 'L1_ffn_W1': _L1_ffn_in['W1'], 'L1_ffn_b1': _L1_ffn_in['b1'], 'L1_ffn_W2': _L1_ffn_in['W2'], 'L1_ffn_b2': _L1_ffn_in['b2'], 'L1_c': _L1_c, 'L1_wmod': _L1_wmod}
    _x0 = _d['L0_attn_hidden_states']
    _d['L0_attn_hidden_states'] = jax.random.normal(jax.random.fold_in(jax.random.key(seed), 1), (2, 1024, 128), dtype=_x0.dtype)
    del _x0
    return _d

def reference(L0_attn_hidden_states, L0_attn_Wq, L0_attn_Wk, L0_attn_Wv, L0_attn_Wo, L0_ffn_gate_w, L0_ffn_w1, L0_ffn_w3, L0_ffn_w2, L0_ffn_e_bias, L0_c, L0_wmod, L1_attn_W_q, L1_attn_b_q, L1_attn_W_k, L1_attn_b_k, L1_attn_W_v, L1_attn_b_v, L1_attn_W_o, L1_attn_b_o, L1_ffn_ln1_w, L1_ffn_ln2_w, L1_ffn_Wq, L1_ffn_bq, L1_ffn_Wk, L1_ffn_bk, L1_ffn_Wv, L1_ffn_bv, L1_ffn_qn_w, L1_ffn_kn_w, L1_ffn_Wg, L1_ffn_bg, L1_ffn_Wo, L1_ffn_bo, L1_ffn_Wr, L1_ffn_br, L1_ffn_W1, L1_ffn_b1, L1_ffn_W2, L1_ffn_b2, L1_c, L1_wmod):

    def _L0_attn_ref(hidden_states, Wq, Wk, Wv, Wo):
        import jax, jax.numpy as jnp
        import numpy as np
        HIDDEN = 128
        NUM_HEADS = 16
        HEAD_DIM = 64
        NUM_KV_HEADS = 4

        def _xavier(key, out_dim, in_dim):
            limit = jnp.sqrt(6.0 / (in_dim + out_dim)).astype(jnp.float32)
            return jax.random.uniform(key, (out_dim, in_dim), jnp.float32, -limit, limit)
        B, S, _ = hidden_states.shape
        q = (hidden_states @ Wq.T).reshape(B, S, NUM_HEADS, HEAD_DIM).transpose(0, 2, 1, 3)
        k = (hidden_states @ Wk.T).reshape(B, S, NUM_KV_HEADS, HEAD_DIM).transpose(0, 2, 1, 3)
        v = (hidden_states @ Wv.T).reshape(B, S, NUM_KV_HEADS, HEAD_DIM).transpose(0, 2, 1, 3)
        n_rep = NUM_HEADS // NUM_KV_HEADS
        if n_rep > 1:
            k = jnp.repeat(k, n_rep, axis=1)
            v = jnp.repeat(v, n_rep, axis=1)
        scale = HEAD_DIM ** (-0.5)
        scores = jnp.einsum('bhqd,bhkd->bhqk', q, k) * scale
        causal = jnp.triu(jnp.full((S, S), -jnp.inf, dtype=scores.dtype), k=1)
        scores = scores + causal[None, None]
        probs = jax.nn.softmax(scores, axis=-1)
        out = jnp.einsum('bhqk,bhkd->bhqd', probs, v)
        out = out.transpose(0, 2, 1, 3).reshape(B, S, NUM_HEADS * HEAD_DIM)
        return out @ Wo.T

    def _L0_ffn_ref(hidden_states, gate_w, w1, w3, w2, e_bias):
        import jax, jax.numpy as jnp
        import numpy as np
        E = 32
        K = 4
        H = 128
        I = 96
        ROUTED_SCALING_FACTOR = 1.0
        orig_shape = hidden_states.shape
        x = hidden_states.reshape(-1, orig_shape[-1])
        T = x.shape[0]
        router_logits = x @ gate_w.T
        scores = jax.nn.sigmoid(router_logits.astype(jnp.float32))
        _, topk_ids = jax.lax.top_k(scores + e_bias[None, :], K)
        topk_w = jnp.take_along_axis(scores, topk_ids, axis=1)
        topk_w = topk_w / jnp.sum(topk_w, axis=1, keepdims=True)
        combine = jnp.zeros((T, E), jnp.float32).at[jnp.arange(T)[:, None], topk_ids].add(topk_w)
        g = jnp.einsum('th,ehi->tei', x, w1)
        u = jnp.einsum('th,ehi->tei', x, w3)
        a = jax.nn.silu(g) * u * combine[:, :, None].astype(x.dtype)
        out = jnp.einsum('tei,eih->th', a, w2)
        out = out * ROUTED_SCALING_FACTOR
        return out.reshape(orig_shape)

    def _L1_attn_ref(x, W_q, b_q, W_k, b_k, W_v, b_v, W_o, b_o):
        import jax, jax.numpy as jnp
        import numpy as np
        EPS = 1e-06
        N_HEADS = 16

        def _heads(t, B, N, H, Dk):
            return t.reshape(B, N, H, Dk).transpose(0, 2, 1, 3)
        B, N, Dm = x.shape
        H = N_HEADS
        Dk = Dm // H
        q = _heads(x @ W_q.T + b_q, B, N, H, Dk)
        k = _heads(x @ W_k.T + b_k, B, N, H, Dk)
        v = _heads(x @ W_v.T + b_v, B, N, H, Dk)
        dec = jnp.exp(-jnp.arange(N, dtype=jnp.float32) / N)[None, None, :, None]
        qf = jax.nn.relu(q) * dec
        kf = jax.nn.relu(k) * dec
        KV = jnp.einsum('bhnd,bhne->bhde', kf, v)
        Ksum = kf.sum(axis=2)
        denom = jnp.einsum('bhnd,bhd->bhn', qf, Ksum) + EPS
        out = jnp.einsum('bhnd,bhde->bhne', qf, KV) / denom[..., None]
        out = out.transpose(0, 2, 1, 3).reshape(B, N, Dm)
        return out @ W_o.T + b_o

    def _L1_ffn_ref(x, ln1_w, ln2_w, Wq, bq, Wk, bk, Wv, bv, qn_w, kn_w, Wg, bg, Wo, bo, Wr, br, W1, b1, W2, b2):
        import jax, jax.numpy as jnp
        import numpy as np
        DIM = 128
        NQ = 16
        NKV = 4
        HD = DIM // NQ
        HID = 256
        E = 8
        B, S = (1, 128)
        EPS = 1e-06

        def rmsnorm(x, w):
            ms = jnp.mean(x * x, axis=-1, keepdims=True)
            return w * (x * jax.lax.rsqrt(ms + EPS))

        def rope_tables(seq_len, head_dim):
            inv_freq = 1.0 / 10000.0 ** (jnp.arange(0, head_dim, 2, dtype=jnp.float32) / head_dim)
            t = jnp.arange(seq_len, dtype=jnp.float32)
            freqs = jnp.einsum('i,j->ij', t, inv_freq)
            return (jnp.cos(freqs), jnp.sin(freqs))

        def apply_rope(x, cos, sin):
            c = cos[None, :, None, :]
            s = sin[None, :, None, :]
            half = x.shape[-1] // 2
            x1, x2 = (x[..., :half], x[..., half:])
            return jnp.concatenate([x1 * c - x2 * s, x1 * s + x2 * c], axis=-1)

        def _forward(x, ln1_w, ln2_w, Wq, bq, Wk, bk, Wv, bv, qn_w, kn_w, Wg, bg, Wo, bo, Wr, br, W1, b1, W2, b2):
            batch, seq, _ = x.shape
            cos, sin = rope_tables(seq, HD)
            h = rmsnorm(x, ln1_w)
            q = (h @ Wq + bq).reshape(batch, seq, NQ, HD)
            k = (h @ Wk + bk).reshape(batch, seq, NKV, HD)
            v = (h @ Wv + bv).reshape(batch, seq, NKV, HD)
            q = rmsnorm(apply_rope(q, cos, sin), qn_w)
            k = rmsnorm(apply_rope(k, cos, sin), kn_w)
            rep = NQ // NKV
            k = jnp.repeat(k, rep, axis=2)
            v = jnp.repeat(v, rep, axis=2)
            scores = jnp.einsum('bthd,bshd->bhts', q, k) / np.sqrt(HD)
            causal = jnp.tril(jnp.ones((seq, seq), dtype=bool))
            scores = jnp.where(causal[None, None], scores, -jnp.inf)
            attn = jax.nn.softmax(scores, axis=-1)
            out = jnp.einsum('bhts,bshd->bthd', attn, v)
            gate = jax.nn.sigmoid(out @ Wg + bg)
            out = (out * gate).reshape(batch, seq, DIM)
            x = x + out @ Wo + bo
            h2 = rmsnorm(x, ln2_w)
            logits = h2 @ Wr + br
            top1 = jnp.argmax(logits, axis=-1).reshape(-1)
            xt = h2.reshape(-1, DIM)
            u = jnp.einsum('td,edf->tef', xt, W1) + b1
            u1, u2 = (u[..., :HID], u[..., HID:])
            act = u1 * jax.nn.sigmoid(u2)
            y_all = jnp.einsum('teh,ehd->ted', act, W2) + b2
            y = jnp.take_along_axis(y_all, top1[:, None, None], axis=1)[:, 0, :]
            return x + y.reshape(batch, seq, DIM)
        return _forward(x, ln1_w, ln2_w, Wq, bq, Wk, bk, Wv, bv, qn_w, kn_w, Wg, bg, Wo, bo, Wr, br, W1, b1, W2, b2)
    x = L0_attn_hidden_states
    mod = (_silu(L0_c) @ L0_wmod).reshape(L0_c.shape[0], 6, 1, -1)
    sa, ca, ga, sb, cb, gb = (mod[:, 0], mod[:, 1], mod[:, 2], mod[:, 3], mod[:, 4], mod[:, 5])
    ga = (2 * (ga >= 0) - 1) * jnp.maximum(jnp.abs(ga), 0.25)
    gb = (2 * (gb >= 0) - 1) * jnp.maximum(jnp.abs(gb), 0.25)
    h = _layernorm(x, axis=-1) * (1 + ca) + sa
    x = x + ga * _L0_attn_ref(h, L0_attn_Wq, L0_attn_Wk, L0_attn_Wv, L0_attn_Wo)
    h = _layernorm(x, axis=-1) * (1 + cb) + sb
    x = x + gb * _L0_ffn_ref(h, L0_ffn_gate_w, L0_ffn_w1, L0_ffn_w3, L0_ffn_w2, L0_ffn_e_bias)
    mod = (_silu(L1_c) @ L1_wmod).reshape(L1_c.shape[0], 6, 1, -1)
    sa, ca, ga, sb, cb, gb = (mod[:, 0], mod[:, 1], mod[:, 2], mod[:, 3], mod[:, 4], mod[:, 5])
    ga = (2 * (ga >= 0) - 1) * jnp.maximum(jnp.abs(ga), 0.25)
    gb = (2 * (gb >= 0) - 1) * jnp.maximum(jnp.abs(gb), 0.25)
    h = _layernorm(x, axis=-1) * (1 + ca) + sa
    x = x + ga * _L1_attn_ref(h, L1_attn_W_q, L1_attn_b_q, L1_attn_W_k, L1_attn_b_k, L1_attn_W_v, L1_attn_b_v, L1_attn_W_o, L1_attn_b_o)
    h = _layernorm(x, axis=-1) * (1 + cb) + sb
    x = x + gb * _L1_ffn_ref(h, L1_ffn_ln1_w, L1_ffn_ln2_w, L1_ffn_Wq, L1_ffn_bq, L1_ffn_Wk, L1_ffn_bk, L1_ffn_Wv, L1_ffn_bv, L1_ffn_qn_w, L1_ffn_kn_w, L1_ffn_Wg, L1_ffn_bg, L1_ffn_Wo, L1_ffn_bo, L1_ffn_Wr, L1_ffn_br, L1_ffn_W1, L1_ffn_b1, L1_ffn_W2, L1_ffn_b2)
    return x

_drawn_inputs = setup_inputs


def setup_inputs(seed=0):
    import zlib

    import numpy as np

    out = dict(_drawn_inputs(seed))
    spreads = {'L1_attn_b_q': (0.0, 0.8),
     'L1_attn_b_k': (0.0, 2.0),
     'L1_attn_b_v': (0.0, 0.489),
     'L1_attn_b_o': (0.0, 0.1),
     'L1_ffn_ln1_w': (1.0, 0.6),
     'L1_ffn_ln2_w': (1.0, 0.2),
     'L1_ffn_bq': (0.0, 0.8),
     'L1_ffn_bk': (0.0, 0.652),
     'L1_ffn_bv': (0.0, 0.1),
     'L1_ffn_qn_w': (1.0, 0.6),
     'L1_ffn_kn_w': (1.0, 0.6),
     'L1_ffn_bg': (0.0, 0.8),
     'L1_ffn_bo': (0.0, 0.1),
     'L1_ffn_br': (0.0, 0.1),
     'L1_ffn_b1': (0.0, 0.542),
     'L1_ffn_b2': (0.0, 0.324)}
    factors = {'L0_attn_Wq': 2.892,
     'L0_attn_Wk': 2.836,
     'L0_ffn_gate_w': 8.0,
     'L0_ffn_w1': 8.0,
     'L0_ffn_w3': 8.0,
     'L0_ffn_w2': 8.0,
     'L0_ffn_e_bias': 8.0,
     'L1_attn_W_q': 8.0,
     'L1_attn_W_k': 8.0,
     'L1_attn_W_v': 8.0,
     'L1_attn_W_o': 4.326,
     'L1_ffn_Wg': 5.752}
    for name, (base, spread) in spreads.items():
        noise = np.random.default_rng([zlib.crc32(name.encode()), seed]).standard_normal(out[name].shape)
        drawn = base * np.exp(spread * noise) if base else spread * noise
        out[name] = jnp.asarray(drawn.astype(out[name].dtype))
    for name, factor in factors.items():
        out[name] = (out[name] * factor).astype(out[name].dtype)
    return out
```

```python
from contextlib import ExitStack

import numpy as np
import concourse.bass as bass
from concourse import mybir

F32 = mybir.dt.float32
F32R = mybir.dt.float32r
BF16 = mybir.dt.bfloat16
U32 = mybir.dt.uint32
ALU = mybir.AluOpType
ACT = mybir.ActivationFunctionType
AX = mybir.AxisListType.X

P = 128
B, S, D = 2, 1024, 128
T = B * S
NT = T // P
NC = T // 512
TPB = S // P
CPB = S // 512
NH, NKV = 16, 4
REP = NH // NKV
MASKED = -1e30
LN_EPS, RMS_EPS = 1e-5, 1e-6


class Core:
    pass


def column(ap, n, inner):
    return ap.unsqueeze(2).broadcast_to((P, n, inner))


def stage_load(nc, k, a):
    with ExitStack() as c:
        sem = lambda n: c.enter_context(nc.semaphore(n))
        sb = lambda n, s, d=F32: c.enter_context(nc.sbuf_tensor(n, s, d))
        loaded, silu_done, mod_done, chain, masks_ready = (sem("ld_loaded"), sem("ld_silu"), sem("ld_mod"),
                                                           sem("ld_chain"), sem("ld_masks"))
        cT = sb("cT", [P, 2, B])
        sig = sb("cT_sig", [P, 2, B])
        wmod = sb("wmod", [P, 2, 6 * D])
        masks = sb("masks_f32", [P, 2, P])
        tmp = sb("mod_tmp", [P, 3, 8])
        loads = [
            (k.x[:, :, :], a["x"].rearrange("b (t p) d -> p (b t) d", p=P)),
            (k.ident[:, :], a["ident"]), (masks[:, :, :], a["masks"]),
            (cT[:, :, :], a["cT"]), (wmod[:, :, :], a["wmod"]),
            (k.dec[:, :], a["dec"]), (k.rope[:, :, :, :], a["rope"]),
            (k.iota[:, :], a["iota"]), (k.headmask[:, :], a["headmask"]), (k.headsel[:, :], a["headsel"]),
            (k.cols[:, :], a["cols"]), (k.rows[:, :], a["rows"].broadcast_to((P, k.rows.shape[1]))),
            (k.wv0[:, :], a["wv0"]), (k.gate0[:, :], a["gate0"]), (k.lin_w[:, :], a["lin_w"]),
            (k.lin_wo[:, :], a["lin_wo"]), (k.ffn_w[:, :], a["ffn_w"]), (k.wg[:, :], a["wg"]),
            (k.wo1[:, :], a["wo1"]), (k.wr[:, :], a["wr"]), (k.b2[:, :], a["b2"]),
        ]
        with nc.Block() as block:
            @block.sync
            def _(sp):
                for dst, src in loads:
                    sp.dma_start(dst, src).then_inc(loaded, 16)

            @block.scalar
            def _(act):
                act.wait_ge(loaded, 16 * len(loads))
                nc.scalar.activation(sig[:, :, :], cT[:, :, :], ACT.Sigmoid).then_inc(silu_done, 1)

            @block.tensor
            def _(pe):
                pe.wait_ge(chain, 2)
                for layer in range(2):
                    for j in range(6):
                        last = nc.tensor.matmul(k.bank(layer)[:, 2 * j:2 * j + 2], wmod[:, layer, j * D:(j + 1) * D],
                                                cT[:, layer, :], start=True, stop=True)
                last.then_inc(mod_done, 1)

            @block.vector
            def _(dve):
                n = [0]

                def link(ins):
                    n[0] += 1
                    ins.then_inc(chain, 1)
                    dve.wait_ge(chain, n[0])

                dve.wait_ge(silu_done, 1)
                link(nc.vector.tensor_copy(k.masks[:, :, :], masks[:, :, :]))
                link(nc.vector.tensor_tensor(cT[:, :, :], cT[:, :, :], sig[:, :, :], ALU.mult))
                link(nc.vector.tensor_copy(k.ident_bf[:, :], k.ident[:, :]))
                link(nc.vector.memset(k.one_col[:, :], 1.0))
                dve.wait_ge(mod_done, 1)
                for layer in range(2):
                    m = k.mod[:, layer, :, :].rearrange("p j b -> p (j b)")
                    link(nc.vector.tensor_copy(m, k.bank(layer)[:, 0:12]))
                    for j in (1, 4):
                        link(nc.vector.tensor_scalar(m[:, 2 * j:2 * j + 2], m[:, 2 * j:2 * j + 2], 1.0, None, ALU.add))
                    for j in (2, 5):
                        g = m[:, 2 * j:2 * j + 2]
                        neg, big, sign = (tmp[:, i, 0:2] for i in range(3))
                        link(nc.vector.tensor_scalar(neg, g, -1.0, None, ALU.mult))
                        link(nc.vector.tensor_tensor(big, g, neg, ALU.max))
                        link(nc.vector.tensor_scalar(big, big, 0.25, None, ALU.max))
                        link(nc.vector.tensor_scalar(sign, g, 0.0, 2.0, ALU.is_ge, ALU.mult))
                        link(nc.vector.scalar_tensor_tensor(out=g, in0=sign, scalar=-1.0, in1=big,
                                                            op0=ALU.add, op1=ALU.mult))


def stage_norm(nc, k, name, src, dst, centred, eps, scale, shift, weight_tiles=None):
    with ExitStack() as c:
        sem = lambda n: c.enter_context(nc.semaphore(name + n))
        sb = lambda n, s, d=F32: c.enter_context(nc.sbuf_tensor(name + n, s, d))
        chain, out_ready = sem("chain"), sem("out")
        var_ready, std_ready, xn_ready, turned, v_done = k.norm_sems
        r, tiles_before = k.norm_uses, k.norm_tiles
        k.norm_uses += 1
        k.norm_tiles += NT if weight_tiles else 0
        st = sb("stats", [P, 4, NT])
        xc, sq = k.tmp0, k.tmp1
        with nc.Block() as block:
            @block.vector
            def _(dve):
                n = [0]

                def link(ins):
                    n[0] += 1
                    ins.then_inc(chain, 1)
                    dve.wait_ge(chain, n[0])

                base = src
                if centred:
                    link(nc.vector.tensor_reduce(st[:, 0, :], src[:, :, :], AX, ALU.add))
                    link(nc.vector.tensor_scalar(st[:, 0, :], st[:, 0, :], 1.0 / D, None, ALU.mult))
                    link(nc.vector.tensor_tensor(xc[:, :, :], src[:, :, :], column(st[:, 0, :], NT, D), ALU.subtract))
                    base = xc
                link(nc.vector.tensor_tensor(sq[:, :, :], base[:, :, :], base[:, :, :], ALU.mult))
                link(nc.vector.tensor_reduce(st[:, 1, :], sq[:, :, :], AX, ALU.add))
                nc.vector.tensor_scalar(st[:, 1, :], st[:, 1, :], 1.0 / D, eps, ALU.mult, ALU.add).then_inc(var_ready, 1)
                dve.wait_ge(std_ready, r + 1)
                link(nc.vector.reciprocal(st[:, 3, :], st[:, 2, :]))
                nc.vector.tensor_tensor(xc[:, :, :], base[:, :, :], column(st[:, 3, :], NT, D),
                                        ALU.mult).then_inc(xn_ready, 1)
                for ch in range(NC):
                    b = ch // CPB
                    dve.wait_ge(turned, NC * r + ch + 1)
                    o = dst[:, ch * 512:(ch + 1) * 512]
                    if shift is None:
                        ins = nc.vector.tensor_scalar(o, k.bank(ch), scale(b), None, ALU.mult)
                    else:
                        ins = nc.vector.tensor_scalar(o, k.bank(ch), scale(b), shift(b), ALU.mult, ALU.add)
                    ins.then_inc(out_ready, 1)
                if weight_tiles:
                    w, width, store = weight_tiles
                    for t in range(NT):
                        dve.wait_ge(v_done, tiles_before + t + 1)
                        store(dve, t, k.bank(4 + t % 4)[:, 0:width]).then_inc(out_ready, 1)

            @block.scalar
            def _(act):
                act.wait_ge(var_ready, r + 1)
                nc.scalar.activation(st[:, 2, :], st[:, 1, :], ACT.Sqrt).then_inc(std_ready, 1)

            @block.tensor
            def _(pe):
                pe.wait_ge(xn_ready, r + 1)
                for t in range(NT):
                    ins = nc.tensor.transpose(k.bank(t // 4)[:, (t % 4) * P:(t % 4 + 1) * P], xc[:, t, :], k.ident[:, :])
                    if t % 4 == 3:
                        ins.then_inc(turned, 1)
                if weight_tiles:
                    w, width, store = weight_tiles
                    pe.wait_ge(out_ready, NC)
                    for t in range(NT):
                        if t >= 4:
                            pe.wait_ge(out_ready, NC + t - 3)
                        nc.tensor.matmul(k.bank(4 + t % 4)[:, 0:width], dst[:, t * P:(t + 1) * P], w,
                                         start=True, stop=True).then_inc(v_done, 1)


def stage_turn(nc, k, name, src, dst, add, pre=None):
    with ExitStack() as c:
        sem = lambda n: c.enter_context(nc.semaphore(name + n))
        ready = sem("ready") if pre else None
        turned, r = k.turn_sem, k.turn_uses
        k.turn_uses += 1
        with nc.Block() as block:
            @block.vector
            def _(dve):
                for ch in range(NC):
                    if pre:
                        pre(dve, ch).then_inc(ready, 1)
                for ch in range(NC):
                    dve.wait_ge(turned, NC * r + ch + 1)
                    o = dst[:, 4 * ch:4 * ch + 4, :]
                    i = k.bank(ch).rearrange("p (t d) -> p t d", t=4)
                    if add:
                        nc.vector.tensor_tensor(o, i, o, ALU.add)
                    else:
                        nc.vector.tensor_copy(o, i)

            @block.tensor
            def _(pe):
                for t in range(NT):
                    if pre and t % 4 == 0:
                        pe.wait_ge(ready, t // 4 + 1)
                    ins = nc.tensor.transpose(k.bank(t // 4)[:, (t % 4) * P:(t % 4 + 1) * P],
                                              src[:, t * P:(t + 1) * P], k.ident[:, :])
                    if t % 4 == 3:
                        ins.then_inc(turned, 1)


def stage_attention(nc, k, name, hd, project, hT, wqk, wo, y, q_dram, k_dram, o_dram):
    G = NKV * B
    scale = float(hd) ** -0.5
    rows1 = 2 * hd if project else 4 * hd + 1
    rows_max = 2 * hd if project else 4 * hd
    NPROJ = CPB * (1 + REP // 2) if project else 0
    NMAX = REP * 12
    NPREP = NPROJ + NMAX + 2
    NFIN = CPB if project else 0
    NSLOT = REP * TPB
    PTR = k.PT.shape[1]
    FIN_SLOT = 29
    NORM_SLOT = 5
    QT = [(qt, ch) for qt in range(TPB) for ch in range(qt // 4 + 1)]

    def plan(prep, fin):
        order = []
        if prep:
            order += [(2 + i // 2, "proj", i) for i in range(NPROJ)]
            order += [(6 + i * 20 // NMAX, "max", i) for i in range(NMAX)]
            order += [(26, "turn", i) for i in range(2)]
        if fin:
            order += [(FIN_SLOT + i, "fin", i) for i in range(NFIN)]
        order.sort(key=lambda x: x[0])
        out = [[] for _ in range(NSLOT)]
        for n, (slot, kind, i) in enumerate(order):
            out[slot].append((kind, i, n))
        return out

    LAST_FIN = max([n for js in plan(True, True) for kind, _, n in js if kind == "fin"], default=0)

    def base(g):
        return NPREP if isinstance(g, int) and g == 0 else (NPREP + NFIN) * g + (NPREP - NFIN)

    def heads(n):
        return TPB * n + PTR

    with ExitStack() as c:
        sem = lambda n: c.enter_context(nc.semaphore(name + n))
        w_full, w_free = sem("w_full"), sem("w_free")
        s_full, p_full = sem("s_full"), sem("p_full")
        pt_free = sem("pt_free")
        oU_full = sem("oU_full")
        q_hi, qb_done, v_done, m_ready = sem("q_hi"), sem("qb_done"), sem("v_done"), sem("m_ready")
        m_row = [sem("m_row0"), sem("m_row1")]
        in_ld = [sem("in_ld0"), sem("in_ld1")]
        wo_ld, sum_ld, rec_done, rec_st, rec_ld = (sem(n) for n in (
            "wo_ld", "sum_ld", "rec_done", "rec_st", "rec_ld"))
        on_done, o_st = sem("on_done"), sem("o_st")
        passed = sem("passed")
        m_set = sem("m_set")
        rec_dram = nc.dram_tensor(name + "rec_dram", (1, REP * S), F32, kind="Internal").ap()
        IN_LD = 16 * (1 if project else 8)
        O = k.ps[:, 6 * 512:8 * 512]

        def W(n):
            return k.bank(n % 2)

        def score_banks(slot):
            first = 2 + 2 * (slot % 2)
            return k.ps[:, first * 512:(first + 2) * 512]

        def steps(eng, step):
            step(0, 0, 0, 0, True, False)
            with eng.Fori(0, (G - 2) // 2) as j:
                step(2 * j + 1, 1, j, j + 1, True, True)
                step(2 * j + 2, 0, j + 1, j + 1, True, True)
            step(G - 1, 1, G // 2 - 1, G // 2, False, True)

        block = c.enter_context(nc.Block())

        @block.tensor
        def _(pe):
            def fill(kind, i, n, par, group, half):
                bank = W(i_of(n))
                n = total(n)
                pe.wait_ge(w_free, n + 1)
                if kind == "proj":
                    if i == 0:
                        pe.wait_ge(in_ld[par], IN_LD * (half + 1))
                    u, ch = divmod(i, CPB)
                    nc.tensor.matmul(bank, k.wqk[:, par, u * P:(u + 1) * P],
                                     hT[:, par * S + ch * 512:par * S + (ch + 1) * 512],
                                     start=True, stop=True).then_inc(w_full, 1)
                elif kind == "max":
                    if i == 0 and project:
                        pe.wait_ge(w_free, n + 2)
                    elif i == 0:
                        pe.wait_ge(in_ld[par], IN_LD * (half + 1))
                    h, j = divmod(i, 12)
                    qt, ch = QT[j]
                    hi = min((ch + 1) * 512, (qt + 1) * P)
                    diagonal = hi == (qt + 1) * P
                    ins = nc.tensor.matmul(bank[:, 0:hi - ch * 512], k.qA[par][0:rows_max, h, qt * P:(qt + 1) * P],
                                           k.kH[par][0:rows_max, ch * 512:hi], start=True, stop=not diagonal)
                    if diagonal:
                        ins = nc.tensor.matmul(bank[:, qt * P - ch * 512:hi - ch * 512], k.ident_bf[:, :],
                                               k.masks[:, 1, :], start=False, stop=True)
                    ins.then_inc(w_full, 1)
                else:
                    pe.wait_ge(m_ready, group + 1)
                    nc.tensor.transpose(bank[0:16, 0:P], k.mmax[:, 16 * i:16 * i + 16],
                                        k.ident[:, :]).then_inc(w_full, 1)

            def fin(i, n, g):
                pe.wait_ge(w_free, total(n) + 1)
                if i == 0:
                    pe.wait_ge(on_done, REP * (g + 1))
                    pe.wait_ge(wo_ld, 16 * g)
                for cc in range(2):
                    ins = nc.tensor.matmul(W(i_of(n)), k.woG[:, cc, :], k.oN[:, cc, i * 512:(i + 1) * 512],
                                           start=(cc == 0), stop=(cc == 1))
                ins.then_inc(w_full, 1)

            def scores(g, par, slot):
                h, kt = divmod(slot, TPB)
                qA, qB, kH, kL = k.qA[par], k.qB[par], k.kH[par], k.kL[par]
                pe.wait_ge(p_full, NSLOT * g + slot + 1)
                region = score_banks(slot)
                for ch in range(kt // 4, CPB):
                    lo, hi = max(ch * 512, kt * P), (ch + 1) * 512
                    diagonal = lo == kt * P
                    ins = nc.tensor.matmul(region[:, lo:hi], kH[0:rows1, kt * P:(kt + 1) * P], qA[0:rows1, h, lo:hi],
                                           start=True, stop=not (project or diagonal))
                    if project:
                        ins = nc.tensor.matmul(region[:, lo:hi], kL[0:hd + 1, kt * P:(kt + 1) * P],
                                               qB[0:hd + 1, h, lo:hi], start=False, stop=not diagonal)
                    if diagonal:
                        ins = nc.tensor.matmul(region[:, lo:lo + P], k.ident_bf[:, :], k.masks[:, 0, :],
                                               start=False, stop=True)
                ins.then_inc(s_full, 1)

            def values(g, par, slot):
                h, kt = divmod(slot, TPB)
                pe.wait_ge(p_full, NSLOT * g + slot + 3)
                for ch in range(kt // 4, CPB):
                    if kt == 0:
                        pe.wait_ge(oU_full, CPB * (REP * g + h) + ch + 1)
                    lo, hi = max(ch * 512, kt * P), (ch + 1) * 512
                    ins = nc.tensor.matmul(O[0:65, lo:hi], k.Vg[par][:, kt, :], k.PT[:, slot % PTR, lo:hi],
                                           start=(kt == 0), stop=(kt == 4 * ch + 3))
                ins.then_inc(pt_free, 1)

            def step(g, par, half, half1, prep, fin_):
                pe.wait_ge(m_row[par], 32 * (half + 1))
                pe.wait_ge(v_done, g + 1)
                if project:
                    pe.wait_ge(qb_done, g + 1)
                scores(g, par, 0)
                jobs = plan(prep, fin_)
                for slot in range(NSLOT):
                    if slot + 1 < NSLOT:
                        scores(g, par, slot + 1)
                    for before in (True, False):
                        for kind, i, n in jobs[slot][:2] if before else jobs[slot][2:]:
                            if kind == "fin":
                                fin(i, (base(g), n), g)
                            else:
                                fill(kind, i, (base(g), n), 1 - par, g + 1, half1)
                        if before:
                            values(g, par, slot)

            for kind, i, n in sum(plan(True, False), []):
                fill(kind, i, (0, n), 0, 0, 0)
            steps(pe, step)
            for i in range(NFIN):
                fin(i, (base(G - 1), NFIN + i), G)

        @block.vector
        def _(dve):
            def consume(kind, i, n, par, group):
                bank = W(i_of(n))
                n = total(n)
                if kind == "proj":
                    dve.wait_ge(q_hi, NPROJ * group + i + 1)
                    u, ch = divmod(i, CPB)
                    cols = slice(ch * 512, (ch + 1) * 512)
                    if u == 0:
                        ins = nc.vector.tensor_tensor(k.kL[par][0:hd, cols], bank[0:hd, :],
                                                      k.kH[par][0:hd, cols].bitcast(F32), ALU.subtract)
                    else:
                        for i in range(2):
                            h = 2 * (u - 1) + i
                            ins = nc.vector.tensor_tensor(k.qA[par][hd:2 * hd, h, cols], bank[i * hd:(i + 1) * hd, :],
                                                          k.qA[par][0:hd, h, cols].bitcast(F32), ALU.subtract)
                elif kind == "max":
                    dve.wait_ge(w_full, n + 1)
                    h, j = divmod(i, 12)
                    qt, ch = QT[j]
                    width = min((ch + 1) * 512, (qt + 1) * P) - ch * 512
                    ins = nc.vector.tensor_reduce(k.mraw[:, ch, h * TPB + qt:h * TPB + qt + 1], bank[:, 0:width],
                                                  AX, ALU.max)
                else:
                    dve.wait_ge(w_full, n + 1)
                    ins = nc.vector.tensor_scalar(k.mT[0:16, i, :], bank[0:16, 0:P], -1.0, None, ALU.mult)
                ins.then_inc(w_free, 1)
                if kind == "max" and i == NMAX - 1:
                    dve.wait_ge(w_free, n + 3)
                    nc.vector.tensor_tensor(k.mmax[:, :], k.mraw[:, 0, :], k.mraw[:, 1, :],
                                            ALU.max).then_inc(m_ready, 1)

            def take_fin(i, n, b):
                dve.wait_ge(w_full, total(n) + 1)
                yc = y[:, b * S + i * 512:b * S + (i + 1) * 512]
                nc.vector.tensor_tensor(yc, W(i_of(n)), yc, ALU.add).then_inc(w_free, 1)

            def copy_out(g, h, ch):
                dve.wait_ge(pt_free, TPB * (REP * g + h) + 4 * (ch + 1) + PTR)
                dve.wait_ge(on_done, REP * g + h + 1)
                cols = slice(ch * 512, (ch + 1) * 512)
                nc.vector.tensor_copy(k.oU[0:65, h, cols], O[0:65, cols]).then_inc(oU_full, 1)

            def recips(g):
                dve.wait_ge(sum_ld, 16 * g)
                nc.vector.reciprocal(k.rs[:, :], k.sm[:, :]).then_inc(rec_done, 1)

            def normalise(g, h):
                if h == 0:
                    dve.wait_ge(rec_ld, 16 * g)
                    if not project:
                        dve.wait_ge(o_st, 16 * g)
                o = k.oN[(h % 2) * hd:(h % 2 + 1) * hd, h // 2, :] if project else k.oN8[0:hd, h, :]
                nc.vector.tensor_tensor(o, k.oU[0:hd, h, :], k.rB[0:hd, h * S:(h + 1) * S], ALU.mult)\
                    .then_inc(on_done, 1)

            def step(g, par, half, half1, prep, fin_):
                jobs = plan(prep, fin_)
                for slot in range(NSLOT):
                    if fin_ and slot == 0:
                        recips(g)
                    if fin_ and slot % TPB == NORM_SLOT:
                        normalise(g, slot // TPB)
                    for kind, i, n in jobs[slot]:
                        if kind == "fin":
                            take_fin(i, (base(g), n), 1 - par)
                        else:
                            consume(kind, i, (base(g), n), 1 - par, g + 1)
                    if slot % TPB >= TPB - CPB:
                        copy_out(g, slot // TPB, slot % TPB - (TPB - CPB))

            dve.sem_inc(w_free, 2)
            dve.sem_inc(oU_full, CPB)
            dve.sem_inc(on_done, REP)
            nc.vector.memset(k.mraw[:, :, :], MASKED).then_inc(m_set, 1)
            dve.wait_ge(m_set, 1)
            ones_row = [k.kL[p][hd:hd + 1, :] if project else k.kH[p][4 * hd:4 * hd + 1, :] for p in range(2)]
            for row in ones_row:
                nc.vector.memset(row.bitcast(F32), 1.0)
            for kind, i, n in sum(plan(True, False), []):
                consume(kind, i, (0, n), 0, 0)
            steps(dve, step)
            recips(G)
            for h in range(REP):
                normalise(G, h)
            for i in range(NFIN):
                take_fin(i, (base(G - 1), NFIN + i), 1)

        @block.scalar
        def _(act):
            def round_high(i, n, par, group):
                if i == 0 and not (isinstance(group, int) and group == 0):
                    act.wait_ge(pt_free, heads(REP * (group - 1)))
                act.wait_ge(w_full, total(n) + 1)
                u, ch = divmod(i, CPB)
                cols = slice(ch * 512, (ch + 1) * 512)
                if u == 0:
                    ins = nc.scalar.copy(k.kH[par][:, cols], W(i_of(n)))
                else:
                    for i in range(2):
                        ins = nc.scalar.copy(k.qA[par][0:hd, 2 * (u - 1) + i, cols], W(i_of(n))[i * hd:(i + 1) * hd, :])
                ins.then_inc(q_hi, 1)

            def step(g, par, half, half1, prep, fin_):
                jobs = plan(prep, fin_)
                for slot in range(NSLOT):
                    kt = slot % TPB
                    act.wait_ge(s_full, NSLOT * g + slot + 1)
                    act.wait_ge(pt_free, NSLOT * g + slot + 1)
                    nc.scalar.activation(k.PT[:, slot % PTR, kt * P:S], score_banks(slot)[:, kt * P:S], ACT.Exp,
                                         scale=scale).then_inc(p_full, 1)
                    for kind, i, n in jobs[slot]:
                        if kind == "proj":
                            round_high(i, (base(g), n), 1 - par, g + 1)

            act.sem_inc(p_full, 2)
            act.sem_inc(pt_free, PTR)
            for kind, i, n in sum(plan(True, False), []):
                if kind == "proj":
                    round_high(i, (0, n), 0, 0)
            steps(act, step)

        @block.gpsimd
        def _(pool):
            def prep_v(group, par, kv):
                if not (isinstance(group, int) and group == 0):
                    pool.wait_ge(pt_free, heads(REP * (group - 1)))
                pool.sem_inc(passed, 1)
                nc.gpsimd.tensor_copy(k.Vg[par][:, :, 0:hd], k.V[:, par * TPB:(par + 1) * TPB,
                                                                bass.ds(kv * hd, hd)]).then_inc(v_done, 1)
                if project:
                    pool.wait_ge(q_hi, NPROJ * (group + 1))
                    pool.sem_inc(passed, 1)
                    nc.gpsimd.tensor_copy(k.qB[par][0:hd, :, :], k.qA[par][0:hd, :, :].bitcast(F32)).then_inc(qb_done, 1)

            def gather_sums(g):
                pool.wait_ge(oU_full, CPB * (REP * g + 1))
                pool.sem_inc(passed, 1)
                pool.dma_start(k.sm[:, :], k.oU[64:65, :, :].rearrange("o h q -> o (h q)")
                               .rearrange("o (p j) -> o p j", p=P)).then_inc(sum_ld, 16)

            def spread(g):
                pool.wait_ge(rec_done, g)
                pool.wait_ge(on_done, REP * g)
                pool.sem_inc(passed, 1)
                pool.dma_start(rec_dram.rearrange("o (p j) -> (o p) j", p=P), k.rs[:, :]).then_inc(rec_st, 16)
                pool.wait_ge(rec_st, 16 * g)
                pool.sem_inc(passed, 1)
                pool.dma_start(k.rB[0:hd, :], rec_dram.broadcast_to((hd, REP * S))).then_inc(rec_ld, 16)

            for p in range(2):
                if not project:
                    nc.gpsimd.memset(k.Vg[p][:, :, hd:64], 0.0)
                nc.gpsimd.memset(k.Vg[p][:, :, 64:65], 1.0)
            prep_v(0, 0, 0)
            prep_v(1, 1, 0)
            gather_sums(1)
            with pool.Fori(0, (G - 2) // 2) as j:
                spread(2 * j + 1)
                prep_v(2 * j + 2, 0, j + 1)
                gather_sums(2 * j + 2)
                spread(2 * j + 2)
                prep_v(2 * j + 3, 1, j + 1)
                gather_sums(2 * j + 3)
            spread(G - 1)
            gather_sums(G)
            spread(G)

        @block.sync
        def _(sp):
            def load(group, par, kv):
                if project:
                    if not (isinstance(group, int) and group < 2):
                        sp.wait_ge(q_hi, NPROJ * (group - 1))
                    sp.dma_start(k.wqk[:, par, :], wqk[bass.ds(kv, 1)].rearrange("o p n -> (o p) n"))\
                        .then_inc(in_ld[par], 16)
                    return
                if not (isinstance(group, int) and group < 2):
                    sp.wait_ge(pt_free, heads(REP * (group - 1)))
                for s in range(4):
                    sp.dma_start(k.qA[par][s * hd:(s + 1) * hd, :, :].bitcast(F32),
                                 q_dram[s % 2, bass.ds(kv * REP, REP), :, par * S:(par + 1) * S]
                                 .rearrange("h d q -> d h q")).then_inc(in_ld[par], 16)
                    sp.dma_start(k.kH[par][s * hd:(s + 1) * hd, :].bitcast(F32),
                                 k_dram[s // 2, bass.ds(kv, 1), :, par * S:(par + 1) * S]
                                 .rearrange("o d q -> (o d) q")).then_inc(in_ld[par], 16)

            def rows(par, last):
                row = k.qB[par][hd:hd + 1, :, :] if project else k.qA[par][4 * hd:4 * hd + 1, :, :]
                row = row.bitcast(F32).rearrange("o h q -> o (h q)")
                for i in range(2):
                    sp.wait_ge(w_free, last + 2 + i)
                    sp.dma_start(row[:, i * 16 * P:(i + 1) * 16 * P].rearrange("o (r c) -> o r c", r=16),
                                 k.mT[0:16, i, :].bitcast(F32)).then_inc(m_row[par], 16)

            def load_wo(kv):
                if project:
                    sp.dma_start(k.woG[:, :, :], wo[bass.ds(kv, 1)].rearrange("o p c n -> (o p) c n"))\
                        .then_inc(wo_ld, 16)

            def store(g, par, kv):
                if not project:
                    sp.wait_ge(on_done, REP * (g + 1))
                    sp.dma_start(o_dram[bass.ds(kv * REP, REP), :, par * S:(par + 1) * S]
                                 .rearrange("h d q -> d h q"), k.oN8[0:hd, :, :]).then_inc(o_st, 16)

            def step(g, par, half, kv_prev):
                load(g + 1, 1 - par, half)
                store(g, 1 - par, kv_prev)
                if project:
                    sp.wait_ge(w_free, base(g) + LAST_FIN + 3)
                load_wo(g_half(g, par, half))
                rows(1 - par, base(g) + NPREP + NFIN - 1)

            def g_half(g, par, half):
                return half - 1 if par == 1 else half

            sp.sem_inc(o_st, 16)
            load(0, 0, 0)
            rows(0, NPREP - 1)
            load(1, 1, 0)
            load_wo(0)
            rows(1, base(0) + NPREP - 1)
            with sp.Fori(0, (G - 2) // 2) as j:
                step(2 * j + 1, 1, j + 1, j)
                step(2 * j + 2, 0, j + 1, j)
            store(G - 1, 0, NKV - 1)
            if project:
                sp.wait_ge(w_free, base(G - 1) + NFIN - 1 + 3)
            load_wo(NKV - 1)
            store(G, 1, NKV - 1)
            if not project:
                sp.wait_ge(o_st, 16 * (G + 1))


def i_of(n):
    return n[1]


def total(n):
    return n[0] + n[1]


def stage_combine(nc, k, name, E, logits, comb_dram, gated, e_bias):
    with ExitStack() as c:
        sem = lambda n: c.enter_context(nc.semaphore(name + n))
        sb = lambda n, s, d=F32: c.enter_context(nc.sbuf_tensor(name + n, s, d))
        chain, scored, weights, turned, copied, stored = (
            sem(n) for n in ("chain", "scored", "weights", "turned", "copied", "stored"))
        score = sb("score", [P, NT, E])
        comb = sb("comb", [P, NT, E])
        pick = sb("pick", [P, NT, E])
        top = sb("top", [P, NT, 8])
        at = sb("at", [P, NT, 8], U32)
        atf = sb("atf", [P, NT, 8])
        tot = sb("tot", [P, 2, NT])
        K = 4 if gated else 1
        with nc.Block() as block:
            if gated:
                @block.scalar
                def _(act):
                    nc.scalar.activation(score[:, :, :], logits[:, :, :], ACT.Sigmoid).then_inc(scored, 1)

            @block.vector
            def _(dve):
                n = [0]

                def link(ins):
                    n[0] += 1
                    ins.then_inc(chain, 1)
                    dve.wait_ge(chain, n[0])

                ranked = logits
                if gated:
                    dve.wait_ge(scored, 1)
                    bias = e_bias.unsqueeze(1).broadcast_to((P, NT, E))
                    link(nc.vector.tensor_tensor(logits[:, :, :], score[:, :, :], bias, ALU.add))
                for t in range(NT):
                    ins = nc.vector.max(top[:, t, :], ranked[:, t, :])
                link(ins)
                for t in range(NT):
                    ins = nc.vector.max_index(at[:, t, :], top[:, t, :], ranked[:, t, :])
                link(ins)
                link(nc.vector.tensor_copy(atf[:, :, :], at[:, :, :]))
                iota = k.iota[:, 0:E].unsqueeze(1).broadcast_to((P, NT, E))
                for r in range(K):
                    o = comb if r == 0 else pick
                    link(nc.vector.tensor_tensor(o[:, :, :], iota, atf[:, :, r:r + 1].broadcast_to((P, NT, E)),
                                                 ALU.is_equal))
                    if r:
                        link(nc.vector.tensor_tensor(comb[:, :, :], comb[:, :, :], pick[:, :, :], ALU.add))
                if gated:
                    link(nc.vector.tensor_tensor(comb[:, :, :], comb[:, :, :], score[:, :, :], ALU.mult))
                    link(nc.vector.tensor_reduce(tot[:, 0, :], comb[:, :, :], AX, ALU.add))
                    link(nc.vector.reciprocal(tot[:, 1, :], tot[:, 0, :]))
                    link(nc.vector.tensor_tensor(comb[:, :, :], comb[:, :, :], column(tot[:, 1, :], NT, E), ALU.mult))
                nc.vector.tensor_copy(pick[:, 0, :], comb[:, 0, :]).then_inc(weights, 1)
                for ch in range(NC):
                    dve.wait_ge(turned, ch + 1)
                    nc.vector.tensor_copy(k.cT[0:E, ch * 512:(ch + 1) * 512], k.bank(ch)[0:E, :]).then_inc(copied, 1)

            @block.tensor
            def _(pe):
                pe.wait_ge(weights, 1)
                for t in range(NT):
                    ins = nc.tensor.transpose(k.bank(t // 4)[0:E, (t % 4) * P:(t % 4 + 1) * P], comb[:, t, :],
                                              k.ident[:, :])
                    if t % 4 == 3:
                        ins.then_inc(turned, 1)

            @block.sync
            def _(sp):
                sp.wait_ge(copied, NC)
                sp.dma_start(comb_dram, k.cT[0:E, :]).then_inc(stored, 16)
                sp.wait_ge(stored, 16)


def stage_experts(nc, k, name, E, M, MT, hT, wa, wb, wd, bias, comb_dram, b2, finish):
    with ExitStack() as c:
        sem = lambda n: c.enter_context(nc.semaphore(name + n))
        sb = lambda n, s, d=F32: c.enter_context(nc.sbuf_tensor(name + n, s, d))
        ld_up = [sem("ldu0"), sem("ldu1")]
        ld_dn = [sem("ldd0"), sem("ldd1")]
        ld = [sem("ld0"), sem("ld1")]
        h_high, h_low = sem("h_high"), sem("h_low")
        w_high, w_low = sem("w_high"), sem("w_low")
        passed = sem("passed")
        f_full, f_high = sem("f_full"), sem("f_high")
        up_full, up_free = sem("up_full"), sem("up_free")
        s_full, a_full, a_free = sem("s_full"), sem("a_full"), sem("a_free")
        seeded, y_full, chain = sem("seeded"), sem("y_full"), sem("chain")
        wUp = sb("wUp", [P, 2, 2 * MT * M])
        wD = sb("wD", [P, 2, MT * D])
        bi = sb("bias", [P, 2, 2 * MT])
        JOBS = NC * MT
        NLD = 16 * (1 + (bias is not None))
        UP = 2 * MT * M
        hH, hL = (k.qA[0][:, 2 * i:2 * i + 2, :].rearrange("p s q -> p (s q)") for i in range(2))
        wf = k.qA[1][:, :, :].rearrange("p s q -> p (s q)")
        wH = [wf[:, par * UP:(par + 1) * UP] for par in range(2)]
        wL = [wf[:, (2 + par) * UP:(3 + par) * UP] for par in range(2)]
        dH = [k.kH[par][0:M, 0:MT * D] for par in range(2)]
        dL = [k.kH[par][0:M, S // 2:S // 2 + MT * D] for par in range(2)]
        fH, fL = (wf[:, (2 + i) * S:(3 + i) * S].rearrange("p (s q) -> p s q", s=2) for i in range(2))
        ACTF = ACT.Silu if bias is None else ACT.Sigmoid

        def up_banks(n):
            return k.bank(2 * (n % 2)), k.bank(2 * (n % 2) + 1)

        def acc(ch):
            return k.bank(4 + ch)

        def pairs(eng, expert):
            expert(0, 0, 0, first=True)
            expert(1, 1, 0)
            with eng.Fori(1, E // 2 - 1) as j:
                expert(2 * j, 0, j)
                expert(2 * j + 1, 1, j)
            expert(E - 2, 0, E // 2 - 1)
            expert(E - 1, 1, E // 2 - 1, last=True)

        with nc.Block() as block:
            @block.sync
            def _(sp):
                def one(x, e):
                    return x[bass.ds(e, 1)].rearrange("o p n -> (o p) n")

                def load_up(e, par):
                    sp.dma_start(wUp[:, par, 0:MT * M], one(wa, e)).then_inc(ld_up[par], 16)
                    sp.dma_start(wUp[:, par, MT * M:UP], one(wb, e)).then_inc(ld_up[par], 16)

                def load_down(e, par):
                    sp.dma_start(wD[0:M, par, :], one(wd, e)).then_inc(ld_dn[par], 16)

                def load(e, par):
                    sp.dma_start(k.cb[0:M, par, :], comb_dram[bass.ds(e, 1), :].broadcast_to((M, T)))\
                        .then_inc(ld[par], 16)
                    if bias is not None:
                        sp.dma_start(bi[:, par, :], one(bias, e)).then_inc(ld[par], 16)

                for e in range(2):
                    load_up(e, e)
                    load_down(e, e)
                load(0, 0)
                load(1, 1)
                with sp.Fori(1, E // 2) as j:
                    for par in range(2):
                        sp.wait_ge(w_low, 2 * (2 * j + par - 1))
                        load_up(2 * j + par, par)
                        load_down(2 * j + par, par)
                        sp.wait_ge(a_free, JOBS * (2 * j + par - 1) + 2)
                        load(2 * j + par, par)

            @block.tensor
            def _(pe):
                def up(e, par, i):
                    ch, m = divmod(i, MT)
                    if i == 0:
                        pe.wait_ge(w_low, 2 * e + 1)
                    pe.wait_ge(up_free, JOBS * e + i + 1)
                    cols = slice(ch * 512, (ch + 1) * 512)
                    for half_ab, bank in enumerate(up_banks(i)):
                        at = half_ab * MT * M + m * M
                        for r, (w, h) in enumerate(((wH, hH), (wH, hL), (wL, hH))):
                            ins = nc.tensor.matmul(bank[0:M, :], w[par][:, at:at + M], h[:, cols],
                                                   start=(r == 0), stop=(r == 2))
                    ins.then_inc(up_full, 1)

                def down(e, par, i):
                    ch, m = divmod(i, MT)
                    if i == 0:
                        pe.wait_ge(w_low, 2 * e + 2)
                    pe.wait_ge(a_full, JOBS * e + i + 1)
                    for w, f in ((dH, fH), (dH, fL), (dL, fH)):
                        ins = nc.tensor.matmul(acc(ch), w[par][:, m * D:(m + 1) * D], f[0:M, i % 2, :],
                                               start=False, stop=False, skip_group_check=True)
                    ins.then_inc(a_free, 1)

                pe.wait_ge(seeded, 1)
                seed_w = b2[:, :] if b2 is not None else k.zero[:, :]
                rows = b2.shape[0] if b2 is not None else 1
                for ch in range(NC):
                    nc.tensor.matmul(acc(ch), seed_w, (k.cT[0:rows, ch * 512:(ch + 1) * 512]),
                                     start=True, stop=False, skip_group_check=True)
                pe.wait_ge(h_low, NC)
                up(0, 0, 0)
                up(0, 0, 1)

                def expert(e, par, half, first=False, last=False):
                    for i in range(JOBS):
                        if i + 2 < JOBS:
                            up(e, par, i + 2)
                        elif not last:
                            up(e + 1, 1 - par, i + 2 - JOBS)
                        if i:
                            down(e, par, i - 1)
                        elif not first:
                            down(e - 1, 1 - par, JOBS - 1)
                pairs(pe, expert)
                down(E - 1, 1, JOBS - 1)
                nc.tensor.matmul(acc(NC - 1), k.zero[:, :], k.cT[0:1, (NC - 1) * 512:NC * 512], start=False, stop=True,
                                 skip_group_check=True).then_inc(y_full, 1)

            @block.scalar
            def _(act):
                def split(e, par, half):
                    act.wait_ge(ld_up[par], 32 * (half + 1))
                    nc.scalar.copy(wH[par], wUp[:, par, :]).then_inc(w_high, 1)

                def split_down(e, par, half):
                    act.wait_ge(ld_dn[par], 16 * (half + 1))
                    nc.scalar.copy(dH[par], wD[0:M, par, :]).then_inc(w_high, 1)

                def high(n, i):
                    act.wait_ge(f_full, n + 1)
                    act.wait_ge(a_free, n + 1)
                    nc.scalar.copy(fH[0:M, i % 2, :], k.hid[0:M, i % 2, :]).then_inc(f_high, 1)

                split(0, 0, 0)
                split_down(0, 0, 0)
                for ch in range(NC):
                    cols = slice(ch * 512, (ch + 1) * 512)
                    nc.scalar.copy(hH[:, cols], hT[:, cols]).then_inc(h_high, 1)

                def expert(e, par, half, first=False, last=False):
                    if bias is not None:
                        act.wait_ge(ld[par], NLD * (half + 1))
                    for i in range(JOBS):
                        m = i % MT
                        act.wait_ge(up_full, JOBS * e + i + 1)
                        if i == 1 and not last:
                            split(e + 1, 1 - par, half + par)
                        if i == 3 and not last:
                            split_down(e + 1, 1 - par, half + par)
                        ga, gb = up_banks(i)
                        if bias is None:
                            ins = nc.scalar.activation(k.gate[0:M, i % 2, :], ga[0:M, :], ACTF)
                        else:
                            ins = nc.scalar.activation(k.gate[0:M, i % 2, :], gb[0:M, :], ACTF,
                                                       bias=bi[0:M, par, MT + m:MT + m + 1])
                        ins.then_inc(s_full, 1)
                        if i or not first:
                            high(JOBS * e + i - 1, i + 1)
                pairs(act, expert)
                high(JOBS * E - 1, 1)

            @block.gpsimd
            def _(pool):
                def low(n, out, whole, high):
                    pool.wait_ge(w_high, n + 1)
                    pool.sem_inc(passed, 1)
                    nc.gpsimd.tensor_tensor(out, whole, high.bitcast(F32), ALU.subtract).then_inc(w_low, 1)

                with pool.Fori(0, E // 2) as j:
                    for par in range(2):
                        low(4 * j + 2 * par, wL[par], wUp[:, par, :], wH[par])
                        low(4 * j + 2 * par + 1, dL[par], wD[0:M, par, :], dH[par])

            @block.vector
            def _(dve):
                dve.sem_inc(up_free, 2)
                dve.sem_inc(a_free, 2)
                nc.vector.memset(k.zero[:, :], 0.0).then_inc(seeded, 1)

                def low(n, i):
                    dve.wait_ge(f_high, n + 1)
                    nc.vector.tensor_tensor(fL[0:M, i % 2, :], k.hid[0:M, i % 2, :], fH[0:M, i % 2, :].bitcast(F32),
                                            ALU.subtract).then_inc(a_full, 1)

                for ch in range(NC):
                    cols = slice(ch * 512, (ch + 1) * 512)
                    dve.wait_ge(h_high, ch + 1)
                    nc.vector.tensor_tensor(hL[:, cols], hT[:, cols], hH[:, cols].bitcast(F32), ALU.subtract)\
                        .then_inc(h_low, 1)

                def expert(e, par, half, first=False, last=False):
                    dve.wait_ge(ld[par], NLD * (half + 1))
                    for i in range(JOBS):
                        ch, m = divmod(i, MT)
                        n = JOBS * e + i
                        dve.wait_ge(s_full, n + 1)
                        ga, gb = up_banks(i)
                        gate = k.gate[0:M, i % 2, :]
                        mul = k.gmul[0:M, i % 2, :]
                        if bias is None:
                            nc.vector.tensor_tensor(mul, gb[0:M, :], gate, ALU.mult).then_inc(up_free, 1)
                        else:
                            nc.vector.scalar_tensor_tensor(out=mul, in0=ga[0:M, :], scalar=bi[0:M, par, m:m + 1],
                                                           in1=gate, op0=ALU.add, op1=ALU.mult).then_inc(up_free, 1)
                        if i or not first:
                            low(n - 1, i + 1)
                        dve.wait_ge(up_free, n + 3)
                        nc.vector.tensor_tensor(k.hid[0:M, i % 2, :], mul, k.cb[0:M, par, ch * 512:(ch + 1) * 512],
                                                ALU.mult).then_inc(f_full, 1)

                pairs(dve, expert)
                low(JOBS * E - 1, 1)
                dve.wait_ge(y_full, 1)
                finish(dve, acc, chain)


def stage_linear(nc, k, hT, y):
    with ExitStack() as c:
        sem = lambda n: c.enter_context(nc.semaphore("lin" + n))
        sb = lambda n, s, d=F32: c.enter_context(nc.sbuf_tensor("lin" + n, s, d))
        proj, taken, chain, kv_full, kv_ready, q_turned, qT_ready, out_full, out_ready, o_turned, oT_ready, y_full = (
            sem(n) for n in ("proj", "taken", "chain", "kv_full", "kv_ready", "q_turned", "qT_ready", "out_full",
                             "out_ready", "o_turned", "oT_ready", "y_full"))
        qkv = k.V2
        KV = sb("KV", [P, B, D + NH])
        qT = k.oU_flat
        oT = k.rB_flat
        den = sb("den", [P, NT, NH])
        rden = sb("rden", [P, NT, NH])
        o = k.tmp0
        with nc.Block() as block:
            @block.tensor
            def _(pe):
                for t in range(NT):
                    if t >= 2:
                        pe.wait_ge(taken, t - 1)
                    nc.tensor.matmul(k.bank(t % 2)[:, 0:3 * D], hT[:, t * P:(t + 1) * P], k.lin_w[:, :],
                                     start=True, stop=True).then_inc(proj, 1)
                pe.wait_ge(taken, NT + 1)
                for b in range(B):
                    for t in range(TPB):
                        tt = b * TPB + t
                        ins = nc.tensor.matmul(k.bank(2 + b)[:, 0:D + 1], qkv[:, tt, D:2 * D], qkv[:, tt, 2 * D:3 * D + 1],
                                               start=(t == 0), stop=(t == TPB - 1))
                    ins.then_inc(kv_full, 1)
                for t in range(NT):
                    ins = nc.tensor.transpose(k.bank(4 + t // 4)[:, (t % 4) * P:(t % 4 + 1) * P], qkv[:, t, 0:D],
                                              k.ident[:, :])
                    if t % 4 == 3:
                        ins.then_inc(q_turned, 1)
                pe.wait_ge(kv_ready, 1)
                pe.wait_ge(qT_ready, NC)
                for t in range(NT):
                    if t >= 2:
                        pe.wait_ge(out_ready, t - 1)
                    nc.tensor.matmul(k.bank(t % 2)[:, 0:D + NH], qT[:, t * P:(t + 1) * P], KV[:, t // TPB, :],
                                     start=True, stop=True).then_inc(out_full, 1)
                pe.wait_ge(out_ready, NT + 1)
                for t in range(NT):
                    ins = nc.tensor.transpose(k.bank(4 + t // 4)[:, (t % 4) * P:(t % 4 + 1) * P], o[:, t, :],
                                              k.ident[:, :])
                    if t % 4 == 3:
                        ins.then_inc(o_turned, 1)
                for ch in range(NC):
                    pe.wait_ge(oT_ready, ch + 1)
                    nc.tensor.matmul(k.bank(ch), k.lin_wo[:, :], oT[:, ch * 512:(ch + 1) * 512],
                                     start=True, stop=True).then_inc(y_full, 1)

            @block.vector
            def _(dve):
                n = [0]

                def link(ins):
                    n[0] += 1
                    ins.then_inc(chain, 1)
                    dve.wait_ge(chain, n[0])

                link(nc.vector.memset(qkv[:, :, 3 * D:3 * D + 1], 1.0))
                for t in range(NT):
                    dve.wait_ge(proj, t + 1)
                    nc.vector.tensor_tensor(qkv[:, t, 0:3 * D], k.bank(t % 2)[:, 0:3 * D], k.row("lin_b"),
                                            ALU.add).then_inc(taken, 1)
                dve.wait_ge(taken, NT)
                qk = qkv[:, :, 0:2 * D]
                link(nc.vector.tensor_scalar(qk, qk, 0.0, None, ALU.max))
                for b in range(B):
                    v = qkv[:, b * TPB:(b + 1) * TPB, 0:2 * D]
                    ins = nc.vector.tensor_tensor(v, v, column(k.dec[:, :], TPB, 2 * D), ALU.mult)
                ins.then_inc(taken, 1)
                for b in range(B):
                    dve.wait_ge(kv_full, b + 1)
                    nc.vector.tensor_tensor(KV[:, b, 0:D], k.bank(2 + b)[:, 0:D], k.headmask[:, :], ALU.mult)
                    ins = nc.vector.tensor_scalar(KV[:, b, D:D + NH], k.headsel[:, :], k.bank(2 + b)[:, D:D + 1], None,
                                                  ALU.mult)
                ins.then_inc(kv_ready, 1)
                for ch in range(NC):
                    dve.wait_ge(q_turned, ch + 1)
                    nc.vector.tensor_copy(qT[:, ch * 512:(ch + 1) * 512], k.bank(4 + ch)).then_inc(qT_ready, 1)
                for t in range(NT):
                    dve.wait_ge(out_full, t + 1)
                    bank = k.bank(t % 2)
                    nc.vector.tensor_scalar(den[:, t, :], bank[:, D:D + NH], RMS_EPS, None, ALU.add)
                    nc.vector.tensor_copy(o[:, t, :], bank[:, 0:D]).then_inc(out_ready, 1)
                dve.wait_ge(out_ready, NT)
                link(nc.vector.reciprocal(rden[:, :, :], den[:, :, :]))
                ov = o[:, :, :].rearrange("p t (h e) -> p (t h) e", h=NH)
                nc.vector.tensor_tensor(ov, ov, column(rden[:, :, :].rearrange("p t h -> p (t h)"), NT * NH, D // NH),
                                        ALU.mult).then_inc(out_ready, 1)
                for ch in range(NC):
                    dve.wait_ge(o_turned, ch + 1)
                    nc.vector.tensor_copy(oT[:, ch * 512:(ch + 1) * 512], k.bank(4 + ch)).then_inc(oT_ready, 1)
                for ch in range(NC):
                    dve.wait_ge(y_full, ch + 1)
                    nc.vector.tensor_scalar(y[:, ch * 512:(ch + 1) * 512], k.bank(ch), k.col("lin_bo"),
                                            k.mod_col(1, 2, ch // CPB), ALU.add, ALU.mult)


def stage_rope(nc, k, qkv, q_dram, k_dram):
    HQK = NH + NKV
    hd = D // NH
    with ExitStack() as c:
        sem = lambda n: c.enter_context(nc.semaphore("rope" + n))
        sb = lambda n, s, d=F32: c.enter_context(nc.sbuf_tensor("rope" + n, s, d))
        chain, var_ready, std_ready, ready, turned, high, low, stored = (
            sem(n) for n in ("chain", "var", "std", "ready", "turned", "high", "low", "stored"))
        r = k.rope_out
        sq = k.rope_sq
        ms = sb("ms", [P, 3, NT * HQK])
        qh = k.qA[0][:, :, :].rearrange("p h q -> p (h q)")
        kh = k.qB[0][0:32, :, :].rearrange("p h q -> p (h q)")
        with nc.Block() as block:
            @block.vector
            def _(dve):
                n = [0]

                def link(ins):
                    n[0] += 1
                    ins.then_inc(chain, 1)
                    dve.wait_ge(chain, n[0])

                for b in range(B):
                    tiles = slice(b * TPB, (b + 1) * TPB)
                    x = qkv[:, tiles, 0:HQK * hd].rearrange("p t (h e) -> p t h e", h=HQK)
                    o = r[:, tiles, :].rearrange("p t (h e) -> p t h e", h=HQK)
                    s = sq[:, tiles, :].rearrange("p t (h e) -> p t h e", h=HQK)
                    cos, sin = (k.rope[:, i, :, :].unsqueeze(2).broadcast_to((P, TPB, HQK, hd // 2)) for i in range(2))
                    lo, hi = slice(0, hd // 2), slice(hd // 2, hd)
                    link(nc.vector.tensor_tensor(o[:, :, :, lo], x[:, :, :, lo], cos, ALU.mult))
                    link(nc.vector.tensor_tensor(o[:, :, :, hi], x[:, :, :, lo], sin, ALU.mult))
                    link(nc.vector.tensor_tensor(s[:, :, :, lo], x[:, :, :, hi], sin, ALU.mult))
                    link(nc.vector.tensor_tensor(s[:, :, :, hi], x[:, :, :, hi], cos, ALU.mult))
                    link(nc.vector.tensor_tensor(o[:, :, :, lo], o[:, :, :, lo], s[:, :, :, lo], ALU.subtract))
                    link(nc.vector.tensor_tensor(o[:, :, :, hi], o[:, :, :, hi], s[:, :, :, hi], ALU.add))
                link(nc.vector.tensor_copy(k.V[:, :, 0:NKV * hd], qkv[:, :, HQK * hd:]))
                link(nc.vector.tensor_tensor(sq[:, :, :], r[:, :, :], r[:, :, :], ALU.mult))
                rv = r[:, :, :].rearrange("p t (h e) -> p (t h) e", h=HQK)
                link(nc.vector.tensor_reduce(ms[:, 0, :], sq[:, :, :].rearrange("p t (h e) -> p (t h) e", h=HQK), AX,
                                             ALU.add))
                nc.vector.tensor_scalar(ms[:, 0, :], ms[:, 0, :], 1.0 / hd, RMS_EPS, ALU.mult, ALU.add)\
                    .then_inc(var_ready, 1)
                dve.wait_ge(std_ready, 1)
                link(nc.vector.reciprocal(ms[:, 2, :], ms[:, 1, :]))
                link(nc.vector.tensor_tensor(rv, rv, column(ms[:, 2, :], NT * HQK, hd), ALU.mult))
                w = k.row("qk_w").unsqueeze(1).broadcast_to((P, NT, HQK * hd))
                nc.vector.tensor_tensor(r[:, :, :], r[:, :, :], w, ALU.mult).then_inc(ready, 1)
                for ch in range(NC):
                    cols = slice(ch * 512, (ch + 1) * 512)
                    lows = slice(T + ch * 512, T + (ch + 1) * 512)
                    dve.wait_ge(high, 2 * ch + 2)
                    nc.vector.tensor_tensor(qh[:, lows], k.bank(ch), qh[:, cols].bitcast(F32), ALU.subtract)\
                        .then_inc(low, 1)
                    nc.vector.tensor_tensor(kh[:, lows], k.bank(4 + ch)[0:32, :], kh[:, cols].bitcast(F32),
                                            ALU.subtract).then_inc(low, 1)

            @block.scalar
            def _(act):
                act.wait_ge(var_ready, 1)
                nc.scalar.activation(ms[:, 1, :], ms[:, 0, :], ACT.Sqrt).then_inc(std_ready, 1)
                for ch in range(NC):
                    cols = slice(ch * 512, (ch + 1) * 512)
                    act.wait_ge(turned, ch + 1)
                    nc.scalar.copy(qh[:, cols], k.bank(ch)).then_inc(high, 1)
                    nc.scalar.copy(kh[:, cols], k.bank(4 + ch)[0:32, :]).then_inc(high, 1)

            @block.tensor
            def _(pe):
                pe.wait_ge(ready, 1)
                for t in range(NT):
                    cols = slice((t % 4) * P, (t % 4 + 1) * P)
                    nc.tensor.transpose(k.bank(t // 4)[:, cols], r[:, t, 0:D], k.ident[:, :])
                    ins = nc.tensor.transpose(k.bank(4 + t // 4)[0:32, cols], r[:, t, D:D + 32], k.ident[:, :])
                    if t % 4 == 3:
                        ins.then_inc(turned, 1)

            @block.sync
            def _(sp):
                sp.wait_ge(low, 2 * NC)
                for part in range(2):
                    cols = slice(part * T, (part + 1) * T)
                    sp.dma_start(q_dram[part].rearrange("h d q -> (h d) q"), qh[:, cols].bitcast(F32)).then_inc(stored, 16)
                    sp.dma_start(k_dram[part].rearrange("h d q -> (h d) q"), kh[:, cols].bitcast(F32)).then_inc(stored, 16)
                sp.wait_ge(stored, 64)


def stage_gate(nc, k, hT, o_dram):
    oT = k.tmp0_flat
    g = k.tmp1_flat
    with ExitStack() as c:
        sem = lambda n: c.enter_context(nc.semaphore("gate" + n))
        loaded, gate_full, gated, prod, out_full = (sem(n) for n in ("ld", "full", "gated", "prod", "out"))
        with nc.Block() as block:
            @block.sync
            def _(sp):
                sp.dma_start(oT[:, :], o_dram.rearrange("h d q -> (h d) q")).then_inc(loaded, 16)

            @block.tensor
            def _(pe):
                pe.wait_ge(loaded, 16)
                for ch in range(NC):
                    nc.tensor.matmul(k.bank(ch), k.wg[:, :], oT[:, ch * 512:(ch + 1) * 512], start=True,
                                     stop=True).then_inc(gate_full, 1)
                for ch in range(NC):
                    pe.wait_ge(prod, ch + 1)
                    nc.tensor.matmul(k.bank(4 + ch), k.wo1[:, :], oT[:, ch * 512:(ch + 1) * 512], start=True,
                                     stop=True).then_inc(out_full, 1)

            @block.scalar
            def _(act):
                for ch in range(NC):
                    act.wait_ge(gate_full, ch + 1)
                    nc.scalar.activation(g[:, ch * 512:(ch + 1) * 512], k.bank(ch), ACT.Sigmoid,
                                         bias=k.col("bg")).then_inc(gated, 1)

            @block.vector
            def _(dve):
                for ch in range(NC):
                    cols = slice(ch * 512, (ch + 1) * 512)
                    dve.wait_ge(gated, ch + 1)
                    nc.vector.tensor_tensor(oT[:, cols], oT[:, cols], g[:, cols], ALU.mult).then_inc(prod, 1)
                for ch in range(NC):
                    cols = slice(ch * 512, (ch + 1) * 512)
                    dve.wait_ge(out_full, ch + 1)
                    nc.vector.scalar_tensor_tensor(out=hT[:, cols], in0=k.bank(4 + ch), scalar=k.col("ffn_bo"),
                                                   in1=hT[:, cols], op0=ALU.add, op1=ALU.add)


def stage_store(nc, k, out):
    with ExitStack() as c:
        stored = c.enter_context(nc.semaphore("out_stored"))
        with nc.Block() as block:
            @block.sync
            def _(sp):
                sp.dma_start(out.rearrange("b (t p) d -> p (b t) d", p=P), k.x[:, :, :]).then_inc(stored, 16)
                sp.wait_ge(stored, 16)


COLS = ["lin_bo", "bg", "ffn_bo", "ln1", "ln2"]
ROWS = [("e_bias", 32), ("lin_b", 3 * D), ("ffn_b", 192), ("qk_w", 160), ("br", 8)]


def program(nc, a, out):
    k = Core()
    with ExitStack() as c:
        sb = lambda n, s, d=F32: c.enter_context(nc.sbuf_tensor(n, s, d))
        k.ps = c.enter_context(nc.psum_tensor("ps", [P, 8 * 512], F32))
        k.bank = lambda i: k.ps[:, i * 512:(i + 1) * 512]
        k.x = sb("x_res", [P, NT, D])
        k.hT = sb("hT", [P, T])
        k.y = sb("y", [P, T])
        k.cT = k.y
        k.qA = [sb(f"qA{p}", [P, REP, S], F32R) for p in range(2)]
        k.qB = [sb(f"qB{p}", [65, REP, S], F32R) for p in range(2)]
        k.kH = [sb(f"kH{p}", [P, S], F32R) for p in range(2)]
        k.kL = [sb(f"kL{p}", [65, S], F32R) for p in range(2)]
        k.Vg = [sb(f"Vg{p}", [P, TPB, 65]) for p in range(2)]
        k.oU = sb("oU", [P, REP, S])
        k.rB = sb("rB", [P, REP * S])
        shared = sb("shared", [P, 8 * S])
        k.V = shared[:, 0:4 * S].rearrange("p (t n) -> p t n", t=NT)
        PTf = shared[:, 4 * S:6 * S]
        k.PT = PTf.rearrange("p (s q) -> p s q", s=2)
        k.oN = shared[:, 6 * S:8 * S].rearrange("p (c q) -> p c q", c=2)
        k.oN8 = shared[0:8, 0:4 * S].rearrange("p (h q) -> p h q", h=REP)
        V1 = shared[:, 6 * S:6 * S + NT * 32].rearrange("p (t n) -> p t n", t=NT)
        k.cb = shared[:, 0:4 * S].rearrange("p (s q) -> p s q", s=2)
        k.gate = PTf[:, 0:S].rearrange("p (s q) -> p s q", s=2)
        k.gmul = PTf[:, S:2 * S].rearrange("p (s q) -> p s q", s=2)
        k.hid = shared[:, 6 * S:7 * S].rearrange("p (s q) -> p s q", s=2)
        k.V2 = shared[:, 0:NT * (3 * D + 1)].rearrange("p (t n) -> p t n", t=NT)
        ffn_qkv = shared[:, 0:NT * 192].rearrange("p (t n) -> p t n", t=NT)
        oUf = k.oU[:, :, :].rearrange("p h q -> p (h q)")
        k.oU_flat = oUf[:, 0:T]
        k.rB_flat = k.rB[:, 0:T]
        k.tmp0_flat = oUf[:, T:2 * T]
        k.tmp0 = k.tmp0_flat.rearrange("p (t d) -> p t d", t=NT)
        k.tmp1_flat = k.rB[:, T:2 * T]
        k.tmp1 = k.tmp1_flat.rearrange("p (t d) -> p t d", t=NT)
        k.rope_out = oUf[:, 0:NT * 160].rearrange("p (t n) -> p t n", t=NT)
        k.rope_sq = k.rB[:, 0:NT * 160].rearrange("p (t n) -> p t n", t=NT)
        k.wqk = sb("wqk", [P, 2, 3 * P])
        k.woG = sb("woG", [P, 2, D])
        k.mraw = sb("mraw", [P, 2, REP * TPB])
        k.mmax = sb("mmax", [P, REP * TPB])
        k.mT = sb("mT", [16, 2, P], F32R)
        k.sm = sb("sm", [P, REP * S // P])
        k.rs = sb("rs", [P, REP * S // P])
        k.ident = sb("ident", [P, P])
        k.ident_bf = sb("ident_bf", [P, P], BF16)
        k.masks = sb("masks", [P, 2, P], BF16)
        k.mod = sb("mod", [P, 2, 6, B])
        k.dec = sb("dec", [P, TPB])
        k.rope = sb("rope", [P, 2, TPB, 4])
        k.iota = sb("iota", [P, 32])
        k.headmask = sb("headmask", [P, D])
        k.headsel = sb("headsel", [P, NH])
        k.cols = sb("cols", [P, len(COLS)])
        k.rows = sb("rows", [P, sum(n for _, n in ROWS)])
        k.one_col = sb("one_col", [P, 1])
        k.zero = sb("zero", [1, P])
        k.wv0 = sb("wv0", [P, 256])
        k.gate0 = sb("gate0", [P, 32])
        k.lin_w = sb("lin_w", [P, 3 * D])
        k.lin_wo = sb("lin_wo", [P, D])
        k.ffn_w = sb("ffn_w", [P, 192])
        k.wg = sb("wg", [P, D])
        k.wo1 = sb("wo1", [P, D])
        k.wr = sb("wr", [P, 8])
        k.b2 = sb("b2", [8, D])
        k.logits = sb("logits", [P, NT, 32])
        starts = {}
        at = 0
        for nme, w in ROWS:
            starts[nme] = (at, w)
            at += w
        k.row = lambda nme: k.rows[:, starts[nme][0]:starts[nme][0] + starts[nme][1]]
        k.col = lambda nme: k.cols[:, COLS.index(nme):COLS.index(nme) + 1]
        k.mod_col = lambda layer, j, b: k.mod[:, layer, j, b:b + 1]
        dram = lambda n, s: nc.dram_tensor(n, s, F32, kind="Internal").ap()
        comb0, comb1 = dram("comb0", (32, T)), dram("comb1", (8, T))
        q_dram, k_dram = dram("q_split", (2, NH, 8, T)), dram("k_split", (2, NKV, 8, T))
        o_dram = dram("o_heads", (NH, 8, T))

        k.norm_sems = [c.enter_context(nc.semaphore("norm_" + n)) for n in ("var", "std", "xn", "turned", "tile")]
        k.turn_sem = c.enter_context(nc.semaphore("turn_turned"))
        k.norm_uses = k.norm_tiles = k.turn_uses = 0

        stage_load(nc, k, a)

        m0 = lambda j: (lambda b: k.mod_col(0, j, b))
        m1 = lambda j: (lambda b: k.mod_col(1, j, b))

        def store_v(dve, t, bank):
            return nc.vector.tensor_copy(k.V[:, t, :], bank)

        stage_norm(nc, k, "n0", k.x, k.hT, True, LN_EPS, m0(1), m0(0), (k.wv0[:, :], 256, store_v))
        with nc.Block() as block:
            @block.gpsimd
            def _(pool):
                nc.gpsimd.memset(k.y[:, :], 0.0)
        stage_attention(nc, k, "a0", 64, True, k.hT, a["wqk0"], a["wo0"], k.y, None, None, None)

        def scale_y(layer, j):
            def pre(dve, ch):
                yc = k.y[:, ch * 512:(ch + 1) * 512]
                return nc.vector.tensor_scalar(yc, yc, k.mod_col(layer, j, ch // CPB), None, ALU.mult)
            return pre

        stage_turn(nc, k, "t0", k.y, k.x, True, scale_y(0, 2))

        def store_logits(E, bias):
            def store(dve, t, bank):
                o = k.logits[:, t, 0:E]
                if bias is None:
                    return nc.vector.tensor_copy(o, bank)
                return nc.vector.tensor_tensor(o, bank, bias, ALU.add)
            return store

        stage_norm(nc, k, "n1", k.x, k.hT, True, LN_EPS, m0(4), m0(3), (k.gate0[:, :], 32, store_logits(32, None)))
        stage_combine(nc, k, "c0", 32, k.logits, comb0, True, k.row("e_bias"))

        def finish0(dve, acc, chain):
            for ch in range(NC):
                nc.vector.tensor_scalar(k.y[:, ch * 512:(ch + 1) * 512], acc(ch), k.mod_col(0, 5, ch // CPB), None,
                                        ALU.mult)

        stage_experts(nc, k, "e0", 32, 96, 1, k.hT, a["w1"], a["w3"], a["w2"], None, comb0, None, finish0)
        stage_turn(nc, k, "t1", k.y, k.x, True)

        stage_norm(nc, k, "n2", k.x, k.hT, True, LN_EPS, m1(1), m1(0))
        stage_linear(nc, k, k.hT, k.y)
        stage_turn(nc, k, "t2", k.y, k.x, True)

        stage_norm(nc, k, "n3", k.x, k.hT, True, LN_EPS, m1(4), m1(3))
        h_tok = k.tmp0
        h1T = k.y
        stage_turn(nc, k, "t3", k.hT, h_tok, False)

        def store_qkv(dve, t, bank):
            return nc.vector.tensor_tensor(ffn_qkv[:, t, :], bank, k.row("ffn_b"), ALU.add)

        stage_norm(nc, k, "n4", h_tok, h1T, False, RMS_EPS, lambda b: k.col("ln1"), None,
                   (k.ffn_w[:, :], 192, store_qkv))
        k.V = V1
        stage_rope(nc, k, ffn_qkv, q_dram, k_dram)
        stage_attention(nc, k, "a1", 8, False, None, None, None, None, q_dram, k_dram, o_dram)
        stage_gate(nc, k, k.hT, o_dram)
        stage_turn(nc, k, "t4", k.hT, h_tok, False)
        h2T = k.rB_flat
        stage_norm(nc, k, "n5", h_tok, h2T, False, RMS_EPS, lambda b: k.col("ln2"), None,
                   (k.wr[:, :], 8, store_logits(8, k.row("br"))))
        stage_combine(nc, k, "c1", 8, k.logits[:, :, 0:8], comb1, False, None)

        def finish1(dve, acc, chain):
            for ch in range(NC):
                yc = k.y[:, ch * 512:(ch + 1) * 512]
                nc.vector.tensor_tensor(yc, acc(ch), k.hT[:, ch * 512:(ch + 1) * 512], ALU.add).then_inc(chain, 1)
                dve.wait_ge(chain, ch + 1)
                nc.vector.tensor_scalar(yc, yc, k.mod_col(1, 5, ch // CPB), None, ALU.mult)

        stage_experts(nc, k, "e1", 8, P, 2, h2T, a["W1a"], a["W1b"], a["W2"], a["b1"], comb1, k.b2, finish1)
        stage_turn(nc, k, "t5", k.y, k.x, True)
        stage_store(nc, k, out)


def constants():
    f = np.float32
    i = np.arange(P)
    hd = D // NH
    masks = np.zeros((P, 2, P), f)
    masks[:, 0, :] = np.where(i[:, None] > i[None, :], MASKED, 0.0)
    masks[:, 1, :] = np.where(i[None, :] > i[:, None], MASKED, 0.0)
    pos = np.arange(S, dtype=f)
    dec = np.exp(-pos / f(S)).astype(f).reshape(TPB, P).T
    inv = (1.0 / f(10000.0) ** (np.arange(0, hd, 2, dtype=f) / f(hd))).astype(f)
    ang = (pos[:, None] * inv[None, :]).astype(f)
    rope = np.stack([np.cos(ang), np.sin(ang)]).astype(f).reshape(2, TPB, P, hd // 2).transpose(2, 0, 1, 3)
    head = i // hd
    return {
        "ident": np.eye(P, dtype=f), "masks": masks, "dec": dec, "rope": rope,
        "iota": np.tile(np.arange(32, dtype=f), (P, 1)),
        "headmask": (head[:, None] == head[None, :]).astype(f),
        "headsel": (head[:, None] == np.arange(NH)[None, :]).astype(f),
    }


def layout(inp):
    g = {n: np.asarray(v) for n, v in inp.items()}
    t = lambda n: g[n].T
    cols = {"lin_bo": g["L1_attn_b_o"], "bg": np.tile(g["L1_ffn_bg"], NH), "ffn_bo": g["L1_ffn_bo"],
            "ln1": g["L1_ffn_ln1_w"], "ln2": g["L1_ffn_ln2_w"]}
    rows = {"e_bias": g["L0_ffn_e_bias"],
            "lin_b": np.concatenate([g["L1_attn_b_q"], g["L1_attn_b_k"], g["L1_attn_b_v"]]),
            "ffn_b": np.concatenate([g["L1_ffn_bq"], g["L1_ffn_bk"], g["L1_ffn_bv"]]),
            "qk_w": np.concatenate([np.tile(g["L1_ffn_qn_w"], NH), np.tile(g["L1_ffn_kn_w"], NKV)]),
            "br": g["L1_ffn_br"]}
    wq = t("L0_attn_Wq").reshape(D, NKV, 2 * P)
    wk = t("L0_attn_Wk").reshape(D, NKV, 64)
    wqk = np.concatenate([wk, wk, wq], axis=2).transpose(1, 0, 2)
    wo0 = t("L0_attn_Wo").reshape(NKV, 2, P, D).transpose(0, 2, 1, 3)
    wg = np.zeros((P, P), g["L1_ffn_Wg"].dtype)
    for h in range(NH):
        wg[8 * h:8 * h + 8, 8 * h:8 * h + 8] = g["L1_ffn_Wg"]
    W1 = g["L1_ffn_W1"]
    return {
        "x": g["L0_attn_hidden_states"],
        "cT": np.stack([t("L0_c"), t("L1_c")], axis=1),
        "wmod": np.stack([g["L0_wmod"], g["L1_wmod"]], axis=1),
        "cols": np.stack([cols[n] for n in COLS], axis=1),
        "rows": np.concatenate([rows[n] for n, _ in ROWS])[None, :],
        "wv0": t("L0_attn_Wv"), "gate0": t("L0_ffn_gate_w"),
        "lin_w": np.concatenate([t("L1_attn_W_q"), t("L1_attn_W_k"), t("L1_attn_W_v")], axis=1),
        "lin_wo": t("L1_attn_W_o"),
        "ffn_w": np.concatenate([g["L1_ffn_Wq"], g["L1_ffn_Wk"], g["L1_ffn_Wv"]], axis=1),
        "wg": wg, "wo1": g["L1_ffn_Wo"], "wr": g["L1_ffn_Wr"], "b2": g["L1_ffn_b2"],
        "wqk0": wqk, "wo0": wo0,
        "w1": g["L0_ffn_w1"], "w3": g["L0_ffn_w3"], "w2": g["L0_ffn_w2"],
        "W1a": W1[:, :, 0:256], "W1b": W1[:, :, 256:512],
        "W2": g["L1_ffn_W2"].reshape(8, 2, P, D).transpose(0, 2, 1, 3).reshape(8, P, 2 * D),
        "b1": g["L1_ffn_b1"].reshape(8, 4, P).transpose(0, 2, 1),
    }


def kernel(**inputs):
    import concourse.bacc as bacc
    from concourse.bass_utils import run_bass_kernel_spmd as run

    nc = bacc.Bacc("TRN2", target_bir_lowering=False, num_devices=1)
    arrays = {n: np.ascontiguousarray(v) for n, v in {**layout(inputs), **constants()}.items()}
    a = {n: nc.dram_tensor("in_" + n, v.shape, mybir.dt.from_np(v.dtype), kind="ExternalInput").ap()
         for n, v in arrays.items()}
    out = nc.dram_tensor("out", arrays["x"].shape, F32, kind="ExternalOutput").ap()
    program(nc, a, out)
    r = run(nc, [{"in_" + n: v for n, v in arrays.items()}], core_ids=[0])
    return r.results[0]["out"]
```

```python
from contextlib import ExitStack

import numpy as np
import concourse.bass as bass
from concourse import mybir

F32 = mybir.dt.float32
F32R = mybir.dt.float32r
BF16 = mybir.dt.bfloat16
U32 = mybir.dt.uint32
ALU = mybir.AluOpType
ACT = mybir.ActivationFunctionType
AX = mybir.AxisListType.X

P = 128
B, S, D = 2, 1024, 128
T = B * S
NT = T // P
NC = T // 512
TPB = S // P
CPB = S // 512
NH, NKV = 16, 4
REP = NH // NKV
MASKED = -1e30
LN_EPS, RMS_EPS = 1e-5, 1e-6


class Core:
    pass


def column(ap, n, inner):
    return ap.unsqueeze(2).broadcast_to((P, n, inner))


def max_jobs():
    jobs = []
    for qt in range(TPB):
        for ch in range(qt // 4 + 1):
            n = 512 // keys_in(qt, ch)
            jobs += [(qt, ch, h, n) for h in range(0, REP, n)]
    return jobs


def keys_in(qt, ch):
    return min((ch + 1) * 512, (qt + 1) * P) - ch * 512


def stage_load(nc, k, a):
    with ExitStack() as c:
        sem = lambda n: c.enter_context(nc.semaphore(n))
        sb = lambda n, s, d=F32: c.enter_context(nc.sbuf_tensor(n, s, d))
        loaded, silu_done, mod_done, chain, masks_ready = (sem("ld_loaded"), sem("ld_silu"), sem("ld_mod"),
                                                           sem("ld_chain"), sem("ld_masks"))
        cT = sb("cT", [P, 2, B])
        sig = sb("cT_sig", [P, 2, B])
        wmod = sb("wmod", [P, 2, 6 * D])
        masks = sb("masks_f32", [P, 2, P])
        tmp = sb("mod_tmp", [P, 3, 8])
        first = [
            (cT[:, :, :], a["cT"]), (wmod[:, 0, :], a["wmod"][:, 0, :]), (k.ident[:, :], a["ident"]),
            (masks[:, :, :], a["masks"]), (wmod[:, 1, :], a["wmod"][:, 1, :]),
            (k.x[:, :, :], a["x"].rearrange("b (t p) d -> p (b t) d", p=P)), (k.wv0[:, :], a["wv0"]),
        ]
        later = [
            (k.dec[:, :], a["dec"]), (k.rope[:, :, :, :], a["rope"]),
            (k.iota[:, :], a["iota"]), (k.headmask[:, :], a["headmask"]), (k.headsel[:, :], a["headsel"]),
            (k.cols[:, :], a["cols"]), (k.rows[:, :], a["rows"].broadcast_to((P, k.rows.shape[1]))),
            (k.gate0[:, :], a["gate0"]), (k.lin_w[:, :], a["lin_w"]),
            (k.lin_wo[:, :], a["lin_wo"]), (k.ffn_w[:, :], a["ffn_w"]), (k.wg[:, :], a["wg"]),
            (k.wo1[:, :], a["wo1"]), (k.wr[:, :], a["wr"]), (k.b2[:, :], a["b2"]),
        ]
        with nc.Block() as block:
            @block.sync
            def _(sp):
                for dst, src in first:
                    sp.dma_start(dst, src).then_inc(loaded, 16)
                for dst, src in later:
                    sp.dma_start(dst, src).then_inc(k.params_ld, 16)
                k.n_params = len(later)

            @block.scalar
            def _(act):
                act.wait_ge(loaded, 16 * len(first))
                nc.scalar.activation(sig[:, :, :], cT[:, :, :], ACT.Sigmoid).then_inc(silu_done, 1)

            @block.tensor
            def _(pe):
                pe.wait_ge(chain, 2)
                for layer in range(2):
                    for j in range(6):
                        last = nc.tensor.matmul(k.bank(layer)[:, 2 * j:2 * j + 2], wmod[:, layer, j * D:(j + 1) * D],
                                                cT[:, layer, :], start=True, stop=True)
                last.then_inc(mod_done, 1)

            @block.vector
            def _(dve):
                n = [0]

                def link(ins):
                    n[0] += 1
                    ins.then_inc(chain, 1)
                    dve.wait_ge(chain, n[0])

                dve.wait_ge(silu_done, 1)
                link(nc.vector.tensor_copy(k.masks[:, :, :], masks[:, :, :]))
                link(nc.vector.tensor_tensor(cT[:, :, :], cT[:, :, :], sig[:, :, :], ALU.mult))
                link(nc.vector.tensor_copy(k.ident_bf[:, :], k.ident[:, :]))
                link(nc.vector.memset(k.one_col[:, :], 1.0))
                dve.wait_ge(mod_done, 1)
                for layer in range(2):
                    m = k.mod[:, layer, :, :].rearrange("p j b -> p (j b)")
                    ins = nc.vector.tensor_copy(m, k.bank(layer)[:, 0:12])
                link(ins)
                scales = k.mod[:, :, 1::3, :]
                link(nc.vector.tensor_scalar(scales, scales, 1.0, None, ALU.add))
                g = k.mod[:, :, 2::3, :]
                neg, big, sign = (tmp[:, i, :].rearrange("p (l j b) -> p l j b", l=2, j=2) for i in range(3))
                link(nc.vector.tensor_scalar(neg, g, -1.0, None, ALU.mult))
                link(nc.vector.tensor_tensor(big, g, neg, ALU.max))
                link(nc.vector.tensor_scalar(big, big, 0.25, None, ALU.max))
                link(nc.vector.tensor_scalar(sign, g, 0.0, 2.0, ALU.is_ge, ALU.mult))
                link(nc.vector.scalar_tensor_tensor(out=g, in0=sign, scalar=-1.0, in1=big,
                                                    op0=ALU.add, op1=ALU.mult))


def stage_norm(nc, k, name, src, dst, centred, eps, scale, shift, weight_tiles=None):
    HT = NT // B
    with ExitStack() as c:
        chain = c.enter_context(nc.semaphore(name + "chain"))
        xc_ready, sq_ready, var_ready, std_ready, xn_ready, turned, out_act, out_dve, v_done, v_stored = k.norm_sems
        r, tiles_before = k.norm_uses, k.norm_tiles
        k.norm_uses += 1
        k.norm_tiles += NT if weight_tiles else 0
        c0 = k.norm_centred
        k.norm_centred += centred
        st = c.enter_context(nc.sbuf_tensor(name + "stats", [P, 4, NT], F32))
        xc, sq = k.tmp0, k.tmp1
        base = xc if centred else src
        halves = [slice(b * HT, (b + 1) * HT) for b in range(B)]
        on_act = [ch for ch in range(NC) if ch != 2]

        def out(ch):
            return dst[:, ch * 512:(ch + 1) * 512]

        def scaled(n_waited):
            if n_waited in on_act:
                return out_act, len(on_act) * r + on_act.index(n_waited) + 1
            return out_dve, r + 1

        with nc.Block() as block:
            @block.vector
            def _(dve):
                n = [0]

                def link(ins):
                    n[0] += 1
                    ins.then_inc(chain, 1)
                    dve.wait_ge(chain, n[0])

                if centred:
                    for t in halves:
                        link(nc.vector.tensor_reduce(st[:, 0, t], src[:, t, :], AX, ALU.add))
                        link(nc.vector.tensor_scalar(st[:, 0, t], st[:, 0, t], 1.0 / D, None, ALU.mult))
                        nc.vector.tensor_tensor(xc[:, t, :], src[:, t, :], column(st[:, 0, t], HT, D),
                                                ALU.subtract).then_inc(xc_ready, 1)
                for b, t in enumerate(halves):
                    dve.wait_ge(sq_ready, B * r + b + 1)
                    link(nc.vector.tensor_reduce(st[:, 1, t], sq[:, t, :], AX, ALU.add))
                    nc.vector.tensor_scalar(st[:, 1, t], st[:, 1, t], 1.0 / D, eps, ALU.mult, ALU.add)\
                        .then_inc(var_ready, 1)
                for b, t in enumerate(halves):
                    dve.wait_ge(std_ready, B * r + b + 1)
                    link(nc.vector.reciprocal(st[:, 3, t], st[:, 2, t]))
                    nc.vector.tensor_tensor(xc[:, t, :], base[:, t, :], column(st[:, 3, t], HT, D),
                                            ALU.mult).then_inc(xn_ready, 1)
                dve.wait_ge(turned, NC * r + 3)
                if shift is None:
                    ins = nc.vector.tensor_scalar(out(2), k.bank(2), scale(1), None, ALU.mult)
                else:
                    ins = nc.vector.tensor_scalar(out(2), k.bank(2), scale(1), shift(1), ALU.mult, ALU.add)
                ins.then_inc(out_dve, 1)
                if weight_tiles:
                    w, width, store = weight_tiles
                    for t in range(NT):
                        dve.wait_ge(v_done, tiles_before + t + 1)
                        store(dve, t, k.bank(4 + t % 4)[:, 0:width]).then_inc(v_stored, 1)

            @block.scalar
            def _(act):
                for b, t in enumerate(halves):
                    if centred:
                        act.wait_ge(xc_ready, B * c0 + b + 1)
                    nc.scalar.activation(sq[:, t, :], base[:, t, :], ACT.Square).then_inc(sq_ready, 1)
                for b, t in enumerate(halves):
                    act.wait_ge(var_ready, B * r + b + 1)
                    nc.scalar.activation(st[:, 2, t], st[:, 1, t], ACT.Sqrt).then_inc(std_ready, 1)
                for ch in on_act:
                    b = ch // CPB
                    act.wait_ge(turned, NC * r + ch + 1)
                    if shift is None:
                        ins = nc.scalar.activation(out(ch), k.bank(ch), ACT.Identity, scale=scale(b))
                    else:
                        ins = nc.scalar.activation(out(ch), k.bank(ch), ACT.Identity, bias=shift(b), scale=scale(b))
                    ins.then_inc(out_act, 1)

            @block.tensor
            def _(pe):
                for t in range(NT):
                    if t % HT == 0:
                        pe.wait_ge(xn_ready, B * r + t // HT + 1)
                    ins = nc.tensor.transpose(k.bank(t // 4)[:, (t % 4) * P:(t % 4 + 1) * P], xc[:, t, :], k.ident[:, :])
                    if t % 4 == 3:
                        ins.then_inc(turned, 1)
                if weight_tiles:
                    w, width, store = weight_tiles
                    for t in range(NT):
                        if t % 4 == 0:
                            pe.wait_ge(*scaled(t // 4))
                        if t >= 4:
                            pe.wait_ge(v_stored, tiles_before + t - 3)
                        nc.tensor.matmul(k.bank(4 + t % 4)[:, 0:width], dst[:, t * P:(t + 1) * P], w,
                                         start=True, stop=True).then_inc(v_done, 1)


def stage_turn(nc, k, name, src, dst, add, pre=None):
    with ExitStack() as c:
        sem = lambda n: c.enter_context(nc.semaphore(name + n))
        ready = sem("ready") if pre else None
        turned, r = k.turn_sem, k.turn_uses
        k.turn_uses += 1
        with nc.Block() as block:
            @block.vector
            def _(dve):
                for ch in range(NC):
                    if pre:
                        pre(dve, ch).then_inc(ready, 1)
                for ch in range(NC):
                    dve.wait_ge(turned, NC * r + ch + 1)
                    o = dst[:, 4 * ch:4 * ch + 4, :]
                    i = k.bank(ch).rearrange("p (t d) -> p t d", t=4)
                    if add:
                        nc.vector.tensor_tensor(o, i, o, ALU.add)
                    else:
                        nc.vector.tensor_copy(o, i)

            @block.tensor
            def _(pe):
                for t in range(NT):
                    if pre and t % 4 == 0:
                        pe.wait_ge(ready, t // 4 + 1)
                    ins = nc.tensor.transpose(k.bank(t // 4)[:, (t % 4) * P:(t % 4 + 1) * P],
                                              src[:, t * P:(t + 1) * P], k.ident[:, :])
                    if t % 4 == 3:
                        ins.then_inc(turned, 1)


def stage_attention64(nc, k, name, hT, wqk, wo, y):
    G = NKV * B
    hd = 64
    scale = float(hd) ** -0.5
    NPROJ = CPB * (1 + REP // 2)
    NMAX = len(max_jobs())
    NPREP = NPROJ + NMAX + 2
    NFIN = CPB
    NSLOT = REP * TPB
    PTR = k.PT.shape[1]
    FIN_SLOT = 29
    NORM_SLOT = 5
    MAX = max_jobs()

    def plan(prep, fin):
        order = []
        if prep:
            order += [(2 + i // 2, "proj", i) for i in range(NPROJ)]
            order += [(6 + i * 20 // NMAX, "max", i) for i in range(NMAX)]
            order += [(26, "turn", i) for i in range(2)]
        if fin:
            order += [(FIN_SLOT + i, "fin", i) for i in range(NFIN)]
        order.sort(key=lambda x: x[0])
        out = [[] for _ in range(NSLOT)]
        for n, (slot, kind, i) in enumerate(order):
            out[slot].append((kind, i, n))
        return out

    LAST_FIN = max([n for js in plan(True, True) for kind, _, n in js if kind == "fin"], default=0)

    def base(g):
        return NPREP if isinstance(g, int) and g == 0 else (NPREP + NFIN) * g + (NPREP - NFIN)

    def heads(n):
        return TPB * n + PTR

    with ExitStack() as c:
        sem = lambda n: c.enter_context(nc.semaphore(name + n))
        w_full, w_free = sem("w_full"), sem("w_free")
        s_full, p_full = sem("s_full"), sem("p_full")
        pt_free = sem("pt_free")
        oU_full = sem("oU_full")
        q_hi, qb_done, v_done, m_ready = sem("q_hi"), sem("qb_done"), sem("v_done"), sem("m_ready")
        m_row = [sem("m_row0"), sem("m_row1")]
        in_ld = [sem("in_ld0"), sem("in_ld1")]
        wo_ld, sum_ld, rec_done, rec_st, rec_ld = (sem(n) for n in (
            "wo_ld", "sum_ld", "rec_done", "rec_st", "rec_ld"))
        on_done = sem("on_done")
        passed = sem("passed")
        m_set = sem("m_set")
        rec_dram = nc.dram_tensor(name + "rec_dram", (1, REP * S), F32, kind="Internal").ap()
        IN_LD = 16
        O = k.ps[:, 6 * 512:8 * 512]

        def W(n):
            return k.bank(n % 2)

        def score_banks(slot):
            first = 2 + 2 * (slot % 2)
            return k.ps[:, first * 512:(first + 2) * 512]

        def steps(eng, step):
            step(0, 0, 0, 0, True, False)
            with eng.Fori(0, (G - 2) // 2) as j:
                step(2 * j + 1, 1, j, j + 1, True, True)
                step(2 * j + 2, 0, j + 1, j + 1, True, True)
            step(G - 1, 1, G // 2 - 1, G // 2, False, True)

        block = c.enter_context(nc.Block())

        @block.tensor
        def _(pe):
            def fill(kind, i, n, par, group, half):
                bank = W(i_of(n))
                n = total(n)
                pe.wait_ge(w_free, n + 1)
                if kind == "proj":
                    if i == 0:
                        pe.wait_ge(in_ld[par], IN_LD * (half + 1))
                    u, ch = divmod(i, CPB)
                    nc.tensor.matmul(bank, k.wqk[:, par, u * P:(u + 1) * P],
                                     hT[:, par * S + ch * 512:par * S + (ch + 1) * 512],
                                     start=True, stop=True).then_inc(w_full, 1)
                elif kind == "max":
                    if i == 0:
                        pe.wait_ge(w_free, n + 2)
                    qt, ch, h0, n_h = MAX[i]
                    width = keys_in(qt, ch)
                    diagonal = ch * 512 + width == (qt + 1) * P
                    for j in range(n_h):
                        ins = nc.tensor.matmul(bank[:, j * width:(j + 1) * width],
                                               k.qA[par][:, h0 + j, qt * P:(qt + 1) * P],
                                               k.kH[par][:, ch * 512:ch * 512 + width], start=True, stop=not diagonal)
                        if diagonal:
                            ins = nc.tensor.matmul(bank[:, (j + 1) * width - P:(j + 1) * width], k.ident_bf[:, :],
                                                   k.masks[:, 1, :], start=False, stop=True)
                    ins.then_inc(w_full, 1)
                else:
                    pe.wait_ge(m_ready, group + 1)
                    nc.tensor.transpose(bank[0:16, 0:P], k.mmax[:, 16 * i:16 * i + 16],
                                        k.ident[:, :]).then_inc(w_full, 1)

            def fin(i, n, g):
                pe.wait_ge(w_free, total(n) + 1)
                if i == 0:
                    pe.wait_ge(on_done, REP * (g + 1))
                    pe.wait_ge(wo_ld, 16 * g)
                for cc in range(2):
                    ins = nc.tensor.matmul(W(i_of(n)), k.woG[:, cc, :], k.oN[:, cc, i * 512:(i + 1) * 512],
                                           start=(cc == 0), stop=(cc == 1))
                ins.then_inc(w_full, 1)

            def scores(g, par, half, slot):
                h, kt = divmod(slot, TPB)
                if slot == 0:
                    pe.wait_ge(m_row[par], 32 * (half + 1))
                    pe.wait_ge(qb_done, g + 1)
                qA, qB, kH, kL = k.qA[par], k.qB[par], k.kH[par], k.kL[par]
                pe.wait_ge(p_full, NSLOT * g + slot + 1)
                region = score_banks(slot)
                for ch in range(kt // 4, CPB):
                    lo, hi = max(ch * 512, kt * P), (ch + 1) * 512
                    diagonal = lo == kt * P
                    nc.tensor.matmul(region[:, lo:hi], kH[:, kt * P:(kt + 1) * P], qA[:, h, lo:hi],
                                     start=True, stop=False)
                    ins = nc.tensor.matmul(region[:, lo:hi], kL[0:hd + 1, kt * P:(kt + 1) * P],
                                           qB[0:hd + 1, h, lo:hi], start=False, stop=not diagonal)
                    if diagonal:
                        ins = nc.tensor.matmul(region[:, lo:lo + P], k.ident_bf[:, :], k.masks[:, 0, :],
                                               start=False, stop=True)
                ins.then_inc(s_full, 1)

            def values(g, par, slot):
                h, kt = divmod(slot, TPB)
                if slot == 0:
                    pe.wait_ge(v_done, g + 1)
                pe.wait_ge(p_full, NSLOT * g + slot + 3)
                for ch in range(kt // 4, CPB):
                    if kt == 0:
                        pe.wait_ge(oU_full, CPB * (REP * g + h) + ch + 1)
                    lo, hi = max(ch * 512, kt * P), (ch + 1) * 512
                    ins = nc.tensor.matmul(O[0:65, lo:hi], k.Vg[par][:, kt, :], k.PT[:, slot % PTR, lo:hi],
                                           start=(kt == 0), stop=(kt == 4 * ch + 3))
                ins.then_inc(pt_free, 1)

            def step(g, par, half, half1, prep, fin_):
                jobs = plan(prep, fin_)
                for slot in range(NSLOT):
                    for place in range(3):
                        if place == 1:
                            if slot + 1 < NSLOT:
                                scores(g, par, half, slot + 1)
                            elif prep:
                                scores(g + 1, 1 - par, half1, 0)
                        if place == 2:
                            values(g, par, slot)
                        for kind, i, n in jobs[slot][place:place + 1] if place < 2 else jobs[slot][2:]:
                            if kind == "fin":
                                fin(i, (base(g), n), g)
                            else:
                                fill(kind, i, (base(g), n), 1 - par, g + 1, half1)

            for kind, i, n in sum(plan(True, False), []):
                fill(kind, i, (0, n), 0, 0, 0)
            scores(0, 0, 0, 0)
            steps(pe, step)
            for i in range(NFIN):
                fin(i, (base(G - 1), NFIN + i), G)

        @block.vector
        def _(dve):
            def consume(kind, i, n, par, group):
                bank = W(i_of(n))
                n = total(n)
                if kind == "proj":
                    dve.wait_ge(q_hi, NPROJ * group + i + 1)
                    u, ch = divmod(i, CPB)
                    cols = slice(ch * 512, (ch + 1) * 512)
                    if u == 0:
                        ins = nc.vector.tensor_tensor(k.kL[par][0:hd, cols], bank[0:hd, :],
                                                      k.kH[par][0:hd, cols].bitcast(F32), ALU.subtract)
                    else:
                        for i in range(2):
                            h = 2 * (u - 1) + i
                            ins = nc.vector.tensor_tensor(k.qA[par][hd:2 * hd, h, cols], bank[i * hd:(i + 1) * hd, :],
                                                          k.qA[par][0:hd, h, cols].bitcast(F32), ALU.subtract)
                elif kind == "max":
                    dve.wait_ge(w_full, n + 1)
                    qt, ch, h0, n_h = MAX[i]
                    out = k.mraw[:, ch, :].rearrange("p (h t) -> p h t", t=TPB)[:, h0:h0 + n_h, qt]
                    width = keys_in(qt, ch)
                    ins = nc.vector.tensor_reduce(out, bank[:, 0:n_h * width].rearrange("p (h w) -> p h w", w=width),
                                                  AX, ALU.max)
                else:
                    dve.wait_ge(w_full, n + 1)
                    ins = nc.vector.tensor_scalar(k.mT[0:16, i, :], bank[0:16, 0:P], -1.0, None, ALU.mult)
                ins.then_inc(w_free, 1)
                if kind == "max" and i == NMAX - 1:
                    dve.wait_ge(w_free, n + 3)
                    nc.vector.tensor_tensor(k.mmax[:, :], k.mraw[:, 0, :], k.mraw[:, 1, :],
                                            ALU.max).then_inc(m_ready, 1)

            def take_fin(i, n, b):
                dve.wait_ge(w_full, total(n) + 1)
                yc = y[:, b * S + i * 512:b * S + (i + 1) * 512]
                nc.vector.tensor_tensor(yc, W(i_of(n)), yc, ALU.add).then_inc(w_free, 1)

            def copy_out(g, h, ch):
                dve.wait_ge(pt_free, TPB * (REP * g + h) + 4 * (ch + 1) + PTR)
                dve.wait_ge(on_done, REP * g + h + 1)
                cols = slice(ch * 512, (ch + 1) * 512)
                nc.vector.tensor_copy(k.oU[0:65, h, cols], O[0:65, cols]).then_inc(oU_full, 1)

            def recips(g):
                dve.wait_ge(sum_ld, 16 * g)
                nc.vector.reciprocal(k.rs[:, :], k.sm[:, :]).then_inc(rec_done, 1)

            def normalise(g, h):
                if h == 0:
                    dve.wait_ge(rec_ld, 16 * g)
                o = k.oN[(h % 2) * hd:(h % 2 + 1) * hd, h // 2, :]
                nc.vector.tensor_tensor(o, k.oU[0:hd, h, :], k.rB[0:hd, h * S:(h + 1) * S], ALU.mult)\
                    .then_inc(on_done, 1)

            def step(g, par, half, half1, prep, fin_):
                jobs = plan(prep, fin_)
                for slot in range(NSLOT):
                    if fin_ and slot == 0:
                        recips(g)
                    if fin_ and slot % TPB == NORM_SLOT:
                        normalise(g, slot // TPB)
                    for kind, i, n in jobs[slot]:
                        if kind == "fin":
                            take_fin(i, (base(g), n), 1 - par)
                        else:
                            consume(kind, i, (base(g), n), 1 - par, g + 1)
                    if slot % TPB >= TPB - CPB:
                        copy_out(g, slot // TPB, slot % TPB - (TPB - CPB))

            dve.sem_inc(w_free, 2)
            dve.sem_inc(oU_full, CPB)
            dve.sem_inc(on_done, REP)
            nc.vector.memset(k.mraw[:, :, :], MASKED).then_inc(m_set, 1)
            dve.wait_ge(m_set, 1)
            for p in range(2):
                nc.vector.memset(k.kL[p][hd:hd + 1, :].bitcast(F32), 1.0)
            for kind, i, n in sum(plan(True, False), []):
                consume(kind, i, (0, n), 0, 0)
            steps(dve, step)
            recips(G)
            for h in range(REP):
                normalise(G, h)
            for i in range(NFIN):
                take_fin(i, (base(G - 1), NFIN + i), 1)

        @block.scalar
        def _(act):
            def round_high(i, n, par, group):
                if i == 0 and not (isinstance(group, int) and group == 0):
                    act.wait_ge(pt_free, heads(REP * (group - 1)))
                act.wait_ge(w_full, total(n) + 1)
                u, ch = divmod(i, CPB)
                cols = slice(ch * 512, (ch + 1) * 512)
                if u == 0:
                    ins = nc.scalar.copy(k.kH[par][:, cols], W(i_of(n)))
                else:
                    for i in range(2):
                        ins = nc.scalar.copy(k.qA[par][0:hd, 2 * (u - 1) + i, cols], W(i_of(n))[i * hd:(i + 1) * hd, :])
                ins.then_inc(q_hi, 1)

            def step(g, par, half, half1, prep, fin_):
                jobs = plan(prep, fin_)
                for slot in range(NSLOT):
                    kt = slot % TPB
                    act.wait_ge(s_full, NSLOT * g + slot + 1)
                    act.wait_ge(pt_free, NSLOT * g + slot + 1)
                    nc.scalar.activation(k.PT[:, slot % PTR, kt * P:S], score_banks(slot)[:, kt * P:S], ACT.Exp,
                                         scale=scale).then_inc(p_full, 1)
                    for kind, i, n in jobs[slot]:
                        if kind == "proj":
                            round_high(i, (base(g), n), 1 - par, g + 1)

            act.sem_inc(p_full, 2)
            act.sem_inc(pt_free, PTR)
            for kind, i, n in sum(plan(True, False), []):
                if kind == "proj":
                    round_high(i, (0, n), 0, 0)
            steps(act, step)

        @block.gpsimd
        def _(pool):
            def prep_v(group, par, kv):
                if not (isinstance(group, int) and group == 0):
                    pool.wait_ge(pt_free, heads(REP * (group - 1)))
                pool.sem_inc(passed, 1)
                nc.gpsimd.tensor_copy(k.Vg[par][:, :, 0:hd], k.V[:, par * TPB:(par + 1) * TPB,
                                                                bass.ds(kv * hd, hd)]).then_inc(v_done, 1)
                pool.wait_ge(q_hi, NPROJ * (group + 1))
                pool.sem_inc(passed, 1)
                nc.gpsimd.tensor_copy(k.qB[par][0:hd, :, :], k.qA[par][0:hd, :, :].bitcast(F32)).then_inc(qb_done, 1)

            def gather_sums(g):
                pool.wait_ge(oU_full, CPB * (REP * g + 1))
                pool.sem_inc(passed, 1)
                pool.dma_start(k.sm[:, :], k.oU[64:65, :, :].rearrange("o h q -> o (h q)")
                               .rearrange("o (p j) -> o p j", p=P)).then_inc(sum_ld, 16)

            def spread(g):
                pool.wait_ge(rec_done, g)
                pool.wait_ge(on_done, REP * g)
                pool.sem_inc(passed, 1)
                pool.dma_start(rec_dram.rearrange("o (p j) -> (o p) j", p=P), k.rs[:, :]).then_inc(rec_st, 16)
                pool.wait_ge(rec_st, 16 * g)
                pool.sem_inc(passed, 1)
                pool.dma_start(k.rB[0:hd, :], rec_dram.broadcast_to((hd, REP * S))).then_inc(rec_ld, 16)

            for p in range(2):
                nc.gpsimd.memset(k.Vg[p][:, :, 64:65], 1.0)
            prep_v(0, 0, 0)
            prep_v(1, 1, 0)
            gather_sums(1)
            with pool.Fori(0, (G - 2) // 2) as j:
                spread(2 * j + 1)
                prep_v(2 * j + 2, 0, j + 1)
                gather_sums(2 * j + 2)
                spread(2 * j + 2)
                prep_v(2 * j + 3, 1, j + 1)
                gather_sums(2 * j + 3)
            spread(G - 1)
            gather_sums(G)
            spread(G)

        @block.sync
        def _(sp):
            def load(group, par, kv):
                if not (isinstance(group, int) and group < 2):
                    sp.wait_ge(q_hi, NPROJ * (group - 1))
                sp.dma_start(k.wqk[:, par, :], wqk[bass.ds(kv, 1)].rearrange("o p n -> (o p) n"))\
                    .then_inc(in_ld[par], 16)

            def rows(par, last):
                row = k.qB[par][hd:hd + 1, :, :].bitcast(F32).rearrange("o h q -> o (h q)")
                for i in range(2):
                    sp.wait_ge(w_free, last + 2 + i)
                    sp.dma_start(row[:, i * 16 * P:(i + 1) * 16 * P].rearrange("o (r c) -> o r c", r=16),
                                 k.mT[0:16, i, :].bitcast(F32)).then_inc(m_row[par], 16)

            def load_wo(kv):
                sp.dma_start(k.woG[:, :, :], wo[bass.ds(kv, 1)].rearrange("o p c n -> (o p) c n"))\
                    .then_inc(wo_ld, 16)

            def step(g, par, half):
                load(g + 1, 1 - par, half)
                rows(1 - par, base(g) + NPREP - 1)
                sp.wait_ge(w_free, base(g) + LAST_FIN + 3)
                load_wo(half - 1 if par == 1 else half)

            load(0, 0, 0)
            rows(0, NPREP - 1)
            load(1, 1, 0)
            load_wo(0)
            rows(1, base(0) + NPREP - 1)
            with sp.Fori(0, (G - 2) // 2) as j:
                step(2 * j + 1, 1, j + 1)
                step(2 * j + 2, 0, j + 1)
            sp.wait_ge(w_free, base(G - 1) + NFIN - 1 + 3)
            load_wo(NKV - 1)


def i_of(n):
    return n[1]


def total(n):
    return n[0] + n[1]


def stage_attention8(nc, k, name, q_dram, k_dram, o_dram, oT):
    G = NKV * B
    hd = D // NH
    scale = float(hd) ** -0.5
    ROWS = 4 * hd
    CT = P // REP
    NMAX = len(max_jobs())
    NPREP = NMAX + 2
    NSLOT = REP * TPB
    PTR = 2 * REP
    MAX = max_jobs()
    RECIP_SLOT, NORM_SLOT, COPY_SLOT = 4, 14, 22
    WARM = 4

    JOBS = [[] for _ in range(NSLOT)]
    for i in range(NMAX):
        JOBS[4 + i * 21 // NMAX].append(("max", i, i))
    for i in range(2):
        JOBS[25].append(("turn", i, NMAX + i))

    def base(g):
        return NPREP * g + NPREP

    with ExitStack() as c:
        sem = lambda n: c.enter_context(nc.semaphore(name + n))
        w_full, w_free = sem("w_full"), sem("w_free")
        s_full, p_full = sem("s_full"), sem("p_full")
        pt_free = sem("pt_free")
        oU_full = sem("oU_full")
        chunk0 = sem("chunk0")
        v_done, m_ready = sem("v_done"), sem("m_ready")
        m_row = [sem("m_row0"), sem("m_row1")]
        in_ld = [sem("in_ld0"), sem("in_ld1")]
        sum_ld, rec_done, rec_st, rec_ld = (sem(n) for n in ("sum_ld", "rec_done", "rec_st", "rec_ld"))
        on_done, o_st = sem("on_done"), sem("o_st")
        passed = sem("passed")
        m_set = sem("m_set")
        oT_ld = sem("oT_ld")
        cleared = sem("cleared")
        rec_dram = nc.dram_tensor(name + "rec_dram", (REP, S), F32, kind="Internal").ap()
        IN_LD = 16 * 6
        O = k.ps[:, 6 * 512:8 * 512]

        def W(n):
            return k.bank(n % 2)

        def score_banks(slot):
            first = 2 + 2 * (slot % 2)
            return k.ps[:, first * 512:(first + 2) * 512]

        def steps(eng, step):
            step(0, 0, 0, first=True)
            with eng.Fori(0, (G - 2) // 2) as j:
                step(2 * j + 1, 1, j + 1)
                step(2 * j + 2, 0, j + 1)
            step(G - 1, 1, G // 2, last=True)

        def groups_read(g):
            return TPB * (g - 1) + 2

        block = c.enter_context(nc.Block())

        @block.tensor
        def _(pe):
            def fill(kind, i, n, first, par, group, half):
                bank = W(n)
                pe.wait_ge(w_free, first + n + 1)
                if kind == "max":
                    if i == 0:
                        pe.wait_ge(in_ld[par], IN_LD * (half + 1))
                    qt, ch, h0, n_h = MAX[i]
                    width = keys_in(qt, ch)
                    diagonal = ch * 512 + width == (qt + 1) * P
                    for j in range(n_h):
                        ins = nc.tensor.matmul(bank[:, j * width:(j + 1) * width],
                                               k.qA[par][:, h0 + j, qt * P:(qt + 1) * P],
                                               k.kL[par][:, ch * 512:ch * 512 + width], start=True, stop=not diagonal)
                        if diagonal:
                            ins = nc.tensor.matmul(bank[:, (j + 1) * width - P:(j + 1) * width], k.ident_bf[:, :],
                                                   k.masks[:, 1, :], start=False, stop=True)
                    ins.then_inc(w_full, 1)
                else:
                    pe.wait_ge(m_ready, group + 1)
                    nc.tensor.transpose(bank[0:16, 0:P], k.mmax[:, 16 * i:16 * i + 16],
                                        k.ident[:, :]).then_inc(w_full, 1)

            def scores(g, par, half, slot):
                kt, h = divmod(slot, REP)
                if slot == 0:
                    pe.wait_ge(m_row[par], 32 * (half + 1))
                pe.wait_ge(p_full, NSLOT * g + slot + 1)
                region = score_banks(slot)
                for ch in range(kt // 4, CPB):
                    lo, hi = max(ch * 512, kt * P), (ch + 1) * 512
                    diagonal = lo == kt * P
                    ins = nc.tensor.matmul(region[:, lo:hi], k.kH[par][:, kt * P:(kt + 1) * P],
                                           k.qA[par][:, h, lo:hi], start=True, stop=not diagonal)
                    if diagonal:
                        ins = nc.tensor.matmul(region[:, lo:lo + P], k.ident_bf[:, :], k.masks[:, 0, :],
                                               start=False, stop=True)
                ins.then_inc(s_full, 1)

            def values(g, par, kt, ch):
                if kt == 0:
                    if ch == 0:
                        pe.wait_ge(v_done, g + 1)
                    pe.wait_ge(oU_full, CPB * g + ch + 1)
                pe.wait_ge(p_full, NSLOT * g + REP * (kt + 1) + 2)
                lo, hi = max(ch * 512, kt * P), (ch + 1) * 512
                for h in range(REP):
                    ins = nc.tensor.matmul(O[CT * h:CT * (h + 1), lo:hi], k.Vg[par][:, kt, 0:CT],
                                           k.PT8[:, (REP * kt + h) % PTR, lo:hi],
                                           start=(kt == 0), stop=(kt == 4 * ch + 3), skip_group_check=True)
                if ch == CPB - 1:
                    ins.then_inc(pt_free, 1)
                elif kt == 3:
                    ins.then_inc(chunk0, 1)

            def idle(g):
                pe.wait_ge(w_free, base(g) + 1)
                nc.tensor.matmul(W(0), k.ident[:, :], k.x[:, 0:4, :], start=True, stop=True)

            def step(g, par, half1, first=False, last=False):
                half = half1 - par if not first else 0
                for slot in range(NSLOT):
                    if slot < 3 and first:
                        idle(g)
                    kt, h = divmod(slot, REP)
                    jobs = [] if last else JOBS[slot]
                    for place in range(3):
                        if place == 1:
                            if slot + 2 < NSLOT:
                                scores(g, par, half, slot + 2)
                            elif not last:
                                scores(g + 1, 1 - par, half1, slot + 2 - NSLOT)
                        if place == 2 and h == REP - 1 and kt < 4:
                            values(g, par, kt, 0)
                        if place == 2 and h == 1 and kt > 0:
                            values(g, par, kt - 1, 1)
                        for kind, i, n in jobs[place:place + 1] if place < 2 else jobs[2:]:
                            fill(kind, i, n, base(g), 1 - par, g + 1, half1)
                values(g, par, TPB - 1, 1)

            for kind, i, n in sum(JOBS, []):
                fill(kind, i, n, 0, 0, 0, 0)
            for i in range(WARM):
                idle(0)
            scores(0, 0, 0, 0)
            scores(0, 0, 0, 1)
            steps(pe, step)

        @block.vector
        def _(dve):
            def consume(kind, i, n, first):
                bank = W(n)
                dve.wait_ge(w_full, first + n + 1)
                if kind == "max":
                    qt, ch, h0, n_h = MAX[i]
                    out = k.mraw[:, ch, :].rearrange("p (h t) -> p h t", t=TPB)[:, h0:h0 + n_h, qt]
                    width = keys_in(qt, ch)
                    ins = nc.vector.tensor_reduce(out, bank[:, 0:n_h * width].rearrange("p (h w) -> p h w", w=width),
                                                  AX, ALU.max)
                else:
                    ins = nc.vector.tensor_scalar(k.mT[0:16, i, :], bank[0:16, 0:P], -1.0, None, ALU.mult)
                ins.then_inc(w_free, 1)
                if kind == "max" and i == NMAX - 1:
                    dve.wait_ge(w_free, first + n + 3)
                    nc.vector.tensor_tensor(k.mmax[:, :], k.mraw[:, 0, :], k.mraw[:, 1, :],
                                            ALU.max).then_inc(m_ready, 1)

            def copy_out(g, ch):
                if ch == 0:
                    dve.wait_ge(chunk0, g + 1)
                else:
                    dve.wait_ge(pt_free, TPB * g + TPB + 2)
                dve.wait_ge(on_done, g + 1)
                cols = slice(ch * 512, (ch + 1) * 512)
                nc.vector.tensor_copy(k.oU8[:, cols], O[:, cols]).then_inc(oU_full, 1)

            def recips(g):
                dve.wait_ge(sum_ld, 16 * REP * g)
                nc.vector.reciprocal(k.rs[:, :], k.sm[:, :]).then_inc(rec_done, 1)

            def normalise(g):
                dve.wait_ge(rec_ld, 16 * REP * g)
                dve.wait_ge(o_st, 16 * REP * g)
                nc.vector.tensor_tensor(k.oN8[:, :], k.oU8[:, :], k.rB[:, 0:S], ALU.mult).then_inc(on_done, 1)

            def step(g, par, half1, first=False, last=False):
                for slot in range(NSLOT):
                    if slot == RECIP_SLOT and not first:
                        recips(g)
                    if slot == NORM_SLOT and not first:
                        normalise(g)
                    if slot == COPY_SLOT:
                        copy_out(g, 0)
                    if not last:
                        for kind, i, n in JOBS[slot]:
                            consume(kind, i, n, base(g))
                copy_out(g, 1)

            dve.sem_inc(w_free, 2)
            dve.sem_inc(oU_full, CPB)
            dve.sem_inc(on_done, 1)
            nc.vector.memset(k.mraw[:, :, :], MASKED).then_inc(m_set, 1)
            dve.wait_ge(m_set, 1)
            for kind, i, n in sum(JOBS, []):
                consume(kind, i, n, 0)
            steps(dve, step)
            recips(G)
            normalise(G)

        @block.scalar
        def _(act):
            def step(g, par, half1, first=False, last=False):
                for slot in range(NSLOT):
                    kt, h = divmod(slot, REP)
                    act.wait_ge(s_full, NSLOT * g + slot + 1)
                    if h == 0:
                        act.wait_ge(pt_free, TPB * g + kt + 1)
                    nc.scalar.activation(k.PT8[:, slot % PTR, kt * P:S], score_banks(slot)[:, kt * P:S], ACT.Exp,
                                         scale=scale).then_inc(p_full, 1)

            act.sem_inc(p_full, 2)
            act.sem_inc(pt_free, 2)
            steps(act, step)

        @block.gpsimd
        def _(pool):
            def prep_v(group, par, kv):
                if not (isinstance(group, int) and group == 0):
                    pool.wait_ge(pt_free, groups_read(group))
                pool.sem_inc(passed, 1)
                nc.gpsimd.tensor_copy(k.Vg[par][:, :, 0:hd], k.V[:, par * TPB:(par + 1) * TPB,
                                                                bass.ds(kv * hd, hd)]).then_inc(v_done, 1)

            nc.gpsimd.memset(k.qA[1][:, :, :].bitcast(F32), 0.0).then_inc(cleared, 1)
            for p in range(2):
                nc.gpsimd.memset(k.Vg[p][:, :, hd:hd + 1], 1.0)
                nc.gpsimd.memset(k.Vg[p][:, :, hd + 1:CT], 0.0)
            prep_v(0, 0, 0)
            prep_v(1, 1, 0)
            with pool.Fori(0, (G - 2) // 2) as j:
                prep_v(2 * j + 2, 0, j + 1)
                prep_v(2 * j + 3, 1, j + 1)

        @block.sync
        def _(sp):
            def load(group, par, kv):
                if not (isinstance(group, int) and group < 2):
                    sp.wait_ge(pt_free, groups_read(group))
                for dst in (k.kL, k.kH):
                    sp.dma_start(dst[par][0:ROWS, :].bitcast(F32), k_dram[bass.ds(kv, 1), :, par * S:(par + 1) * S]
                                 .rearrange("o d q -> (o d) q")).then_inc(in_ld[par], 16)
                for s in range(4):
                    sp.dma_start(k.qA[par][s * hd:(s + 1) * hd, :, :].bitcast(F32),
                                 q_dram[s % 2, bass.ds(kv * REP, REP), :, par * S:(par + 1) * S]
                                 .rearrange("h d q -> d h q")).then_inc(in_ld[par], 16)

            def rows(par, last):
                row = k.qA[par][ROWS:ROWS + 1, :, :].bitcast(F32).rearrange("o h q -> o (h q)")
                for i in range(2):
                    sp.wait_ge(w_free, last + 2 + i)
                    sp.dma_start(row[:, i * 16 * P:(i + 1) * 16 * P].rearrange("o (r c) -> o r c", r=16),
                                 k.mT[0:16, i, :].bitcast(F32)).then_inc(m_row[par], 16)

            def store(g, par, kv):
                sp.wait_ge(on_done, g + 1)
                for h in range(REP):
                    sp.dma_start(o_dram[bass.ds(kv * REP + h, 1), :, par * S:(par + 1) * S]
                                 .rearrange("o d q -> (o d) q"), k.oN8[CT * h:CT * h + hd, :]).then_inc(o_st, 16)

            def gather_sums(g):
                sp.wait_ge(oU_full, CPB * g + CPB)
                for h in range(REP):
                    row = CT * h + hd
                    sp.dma_start(k.sm[CT * h:CT * (h + 1), :], k.oU8[row:row + 1, :]
                                   .rearrange("o (p j) -> o p j", p=CT)).then_inc(sum_ld, 16)

            def spread(g):
                sp.wait_ge(rec_done, g)
                sp.wait_ge(on_done, g)
                sp.dma_start(rec_dram.rearrange("h (p j) -> (h p) j", p=CT), k.rs[:, :]).then_inc(rec_st, 16)
                sp.wait_ge(rec_st, 16 * g)
                for h in range(REP):
                    sp.dma_start(k.rB[CT * h:CT * (h + 1), 0:S], rec_dram[h:h + 1, :].broadcast_to((CT, S)))\
                        .then_inc(rec_ld, 16)

            def step(g, par, half, kv_prev):
                load(g + 1, 1 - par, half)
                gather_sums(g)
                spread(g)
                store(g, 1 - par, kv_prev)
                rows(1 - par, base(g) + NPREP - 1)

            sp.sem_inc(o_st, 16 * REP)
            load(0, 0, 0)
            sp.wait_ge(cleared, 1)
            load(1, 1, 0)
            rows(0, NPREP - 1)
            rows(1, base(0) + NPREP - 1)
            with sp.Fori(0, (G - 2) // 2) as j:
                step(2 * j + 1, 1, j + 1, j)
                step(2 * j + 2, 0, j + 1, j)
            gather_sums(G - 1)
            spread(G - 1)
            store(G - 1, 0, NKV - 1)
            gather_sums(G)
            spread(G)
            for b in range(B):
                if b == B - 1:
                    store(G, 1, NKV - 1)
                sp.wait_ge(o_st, 16 * REP * (G + b))
                sp.dma_start(oT[:, b * S:(b + 1) * S], o_dram[:, :, b * S:(b + 1) * S]
                             .rearrange("h d q -> (h d) q")).then_inc(oT_ld, 16)
            sp.wait_ge(oT_ld, 16 * B)


def stage_combine(nc, k, name, E, logits, comb_dram, gated, e_bias):
    with ExitStack() as c:
        sem = lambda n: c.enter_context(nc.semaphore(name + n))
        sb = lambda n, s, d=F32: c.enter_context(nc.sbuf_tensor(name + n, s, d))
        chain, scored, weights, turned, copied, stored = (
            sem(n) for n in ("chain", "scored", "weights", "turned", "copied", "stored"))
        score = sb("score", [P, NT, E])
        comb = sb("comb", [P, NT, E])
        pick = sb("pick", [P, NT, E])
        top = sb("top", [P, NT, 8])
        at = sb("at", [P, NT, 8], U32)
        atf = sb("atf", [P, NT, 8])
        tot = sb("tot", [P, 2, NT])
        K = 4 if gated else 1
        with nc.Block() as block:
            if gated:
                @block.scalar
                def _(act):
                    nc.scalar.activation(score[:, :, :], logits[:, :, :], ACT.Sigmoid).then_inc(scored, 1)

            @block.vector
            def _(dve):
                n = [0]

                def link(ins):
                    n[0] += 1
                    ins.then_inc(chain, 1)
                    dve.wait_ge(chain, n[0])

                ranked = logits
                if gated:
                    dve.wait_ge(scored, 1)
                    bias = e_bias.unsqueeze(1).broadcast_to((P, NT, E))
                    link(nc.vector.tensor_tensor(logits[:, :, :], score[:, :, :], bias, ALU.add))
                for t in range(NT):
                    ins = nc.vector.max(top[:, t, :], ranked[:, t, :])
                link(ins)
                for t in range(NT):
                    ins = nc.vector.max_index(at[:, t, :], top[:, t, :], ranked[:, t, :])
                link(ins)
                link(nc.vector.tensor_copy(atf[:, :, :], at[:, :, :]))
                iota = k.iota[:, 0:E].unsqueeze(1).broadcast_to((P, NT, E))
                for r in range(K):
                    o = comb if r == 0 else pick
                    link(nc.vector.tensor_tensor(o[:, :, :], iota, atf[:, :, r:r + 1].broadcast_to((P, NT, E)),
                                                 ALU.is_equal))
                    if r:
                        link(nc.vector.tensor_tensor(comb[:, :, :], comb[:, :, :], pick[:, :, :], ALU.add))
                if gated:
                    link(nc.vector.tensor_tensor(comb[:, :, :], comb[:, :, :], score[:, :, :], ALU.mult))
                    link(nc.vector.tensor_reduce(tot[:, 0, :], comb[:, :, :], AX, ALU.add))
                    link(nc.vector.reciprocal(tot[:, 1, :], tot[:, 0, :]))
                    link(nc.vector.tensor_tensor(comb[:, :, :], comb[:, :, :], column(tot[:, 1, :], NT, E), ALU.mult))
                nc.vector.tensor_copy(pick[:, 0, :], comb[:, 0, :]).then_inc(weights, 1)
                for ch in range(NC):
                    dve.wait_ge(turned, ch + 1)
                    nc.vector.tensor_copy(k.cT[0:E, ch * 512:(ch + 1) * 512], k.bank(ch)[0:E, :]).then_inc(copied, 1)

            @block.tensor
            def _(pe):
                pe.wait_ge(weights, 1)
                for t in range(NT):
                    ins = nc.tensor.transpose(k.bank(t // 4)[0:E, (t % 4) * P:(t % 4 + 1) * P], comb[:, t, :],
                                              k.ident[:, :])
                    if t % 4 == 3:
                        ins.then_inc(turned, 1)

            @block.sync
            def _(sp):
                sp.wait_ge(copied, NC)
                sp.dma_start(comb_dram, k.cT[0:E, :]).then_inc(stored, 16)
                sp.wait_ge(stored, 16)


def stage_experts(nc, k, name, E, M, MT, hT, wa, wb, wd, bias, comb_dram, b2, finish):
    with ExitStack() as c:
        sem = lambda n: c.enter_context(nc.semaphore(name + n))
        sb = lambda n, s, d=F32: c.enter_context(nc.sbuf_tensor(name + n, s, d))
        ld_up = [sem("ldu0"), sem("ldu1")]
        ld_dn = [sem("ldd0"), sem("ldd1")]
        ld = [sem("ld0"), sem("ld1")]
        h_high, h_low = sem("h_high"), sem("h_low")
        w_high, w_low = sem("w_high"), sem("w_low")
        passed = sem("passed")
        f_full, f_high = sem("f_full"), sem("f_high")
        up_full, up_free = sem("up_full"), sem("up_free")
        s_full, a_full, a_free = sem("s_full"), sem("a_full"), sem("a_free")
        seeded, y_full, chain = sem("seeded"), sem("y_full"), sem("chain")
        wUp = sb("wUp", [P, 2, 2 * MT * M])
        wD = sb("wD", [P, 2, MT * D])
        bi = sb("bias", [P, 2, 2 * MT])
        JOBS = NC * MT
        NLD = 16 * (1 + (bias is not None))
        UP = 2 * MT * M
        hH, hL = (k.qA[0][:, 2 * i:2 * i + 2, :].rearrange("p s q -> p (s q)") for i in range(2))
        wf = k.qA[1][:, :, :].rearrange("p s q -> p (s q)")
        wH = [wf[:, par * UP:(par + 1) * UP] for par in range(2)]
        wL = [wf[:, (2 + par) * UP:(3 + par) * UP] for par in range(2)]
        dH = [k.kH[par][0:M, 0:MT * D] for par in range(2)]
        dL = [k.kH[par][0:M, S // 2:S // 2 + MT * D] for par in range(2)]
        fH, fL = (wf[:, (2 + i) * S:(3 + i) * S].rearrange("p (s q) -> p s q", s=2) for i in range(2))
        ACTF = ACT.Silu if bias is None else ACT.Sigmoid

        def up_banks(n):
            return k.bank(2 * (n % 2)), k.bank(2 * (n % 2) + 1)

        def acc(ch):
            return k.bank(4 + ch)

        def pairs(eng, expert):
            expert(0, 0, 0, first=True)
            expert(1, 1, 0)
            with eng.Fori(1, E // 2 - 1) as j:
                expert(2 * j, 0, j)
                expert(2 * j + 1, 1, j)
            expert(E - 2, 0, E // 2 - 1)
            expert(E - 1, 1, E // 2 - 1, last=True)

        with nc.Block() as block:
            @block.sync
            def _(sp):
                def one(x, e):
                    return x[bass.ds(e, 1)].rearrange("o p n -> (o p) n")

                def load_up(e, par):
                    sp.dma_start(wUp[:, par, 0:MT * M], one(wa, e)).then_inc(ld_up[par], 16)
                    sp.dma_start(wUp[:, par, MT * M:UP], one(wb, e)).then_inc(ld_up[par], 16)

                def load_down(e, par):
                    sp.dma_start(wD[0:M, par, :], one(wd, e)).then_inc(ld_dn[par], 16)

                def load(e, par):
                    sp.dma_start(k.cb[0:M, par, :], comb_dram[bass.ds(e, 1), :].broadcast_to((M, T)))\
                        .then_inc(ld[par], 16)
                    if bias is not None:
                        sp.dma_start(bi[:, par, :], one(bias, e)).then_inc(ld[par], 16)

                for e in range(2):
                    load_up(e, e)
                    load_down(e, e)
                load(0, 0)
                load(1, 1)
                with sp.Fori(1, E // 2) as j:
                    for par in range(2):
                        sp.wait_ge(w_low, 2 * (2 * j + par - 1))
                        load_up(2 * j + par, par)
                        load_down(2 * j + par, par)
                        sp.wait_ge(a_free, JOBS * (2 * j + par - 1) + 2)
                        load(2 * j + par, par)

            @block.tensor
            def _(pe):
                def up(e, par, i):
                    ch, m = divmod(i, MT)
                    if i == 0:
                        pe.wait_ge(w_low, 2 * e + 1)
                    pe.wait_ge(up_free, JOBS * e + i + 1)
                    cols = slice(ch * 512, (ch + 1) * 512)
                    for half_ab, bank in enumerate(up_banks(i)):
                        at = half_ab * MT * M + m * M
                        for r, (w, h) in enumerate(((wH, hH), (wH, hL), (wL, hH))):
                            ins = nc.tensor.matmul(bank[0:M, :], w[par][:, at:at + M], h[:, cols],
                                                   start=(r == 0), stop=(r == 2))
                    ins.then_inc(up_full, 1)

                def down(e, par, i):
                    ch, m = divmod(i, MT)
                    if i == 0:
                        pe.wait_ge(w_low, 2 * e + 2)
                    pe.wait_ge(a_full, JOBS * e + i + 1)
                    for w, f in ((dH, fH), (dH, fL), (dL, fH)):
                        ins = nc.tensor.matmul(acc(ch), w[par][:, m * D:(m + 1) * D], f[0:M, i % 2, :],
                                               start=False, stop=False, skip_group_check=True)
                    ins.then_inc(a_free, 1)

                pe.wait_ge(seeded, 1)
                seed_w = b2[:, :] if b2 is not None else k.zero[:, :]
                rows = b2.shape[0] if b2 is not None else 1
                for ch in range(NC):
                    nc.tensor.matmul(acc(ch), seed_w, (k.cT[0:rows, ch * 512:(ch + 1) * 512]),
                                     start=True, stop=False, skip_group_check=True)
                pe.wait_ge(h_low, NC)
                up(0, 0, 0)
                up(0, 0, 1)

                def expert(e, par, half, first=False, last=False):
                    for i in range(JOBS):
                        if i + 2 < JOBS:
                            up(e, par, i + 2)
                        elif not last:
                            up(e + 1, 1 - par, i + 2 - JOBS)
                        if i:
                            down(e, par, i - 1)
                        elif not first:
                            down(e - 1, 1 - par, JOBS - 1)
                pairs(pe, expert)
                down(E - 1, 1, JOBS - 1)
                nc.tensor.matmul(acc(NC - 1), k.zero[:, :], k.cT[0:1, (NC - 1) * 512:NC * 512], start=False, stop=True,
                                 skip_group_check=True).then_inc(y_full, 1)

            @block.scalar
            def _(act):
                def split(e, par, half):
                    act.wait_ge(ld_up[par], 32 * (half + 1))
                    nc.scalar.copy(wH[par], wUp[:, par, :]).then_inc(w_high, 1)

                def split_down(e, par, half):
                    act.wait_ge(ld_dn[par], 16 * (half + 1))
                    nc.scalar.copy(dH[par], wD[0:M, par, :]).then_inc(w_high, 1)

                def high(n, i):
                    act.wait_ge(f_full, n + 1)
                    act.wait_ge(a_free, n + 1)
                    nc.scalar.copy(fH[0:M, i % 2, :], k.hid[0:M, i % 2, :]).then_inc(f_high, 1)

                split(0, 0, 0)
                split_down(0, 0, 0)
                for ch in range(NC):
                    cols = slice(ch * 512, (ch + 1) * 512)
                    nc.scalar.copy(hH[:, cols], hT[:, cols]).then_inc(h_high, 1)

                def expert(e, par, half, first=False, last=False):
                    if bias is not None:
                        act.wait_ge(ld[par], NLD * (half + 1))
                    for i in range(JOBS):
                        m = i % MT
                        act.wait_ge(up_full, JOBS * e + i + 1)
                        if i == 1 and not last:
                            split(e + 1, 1 - par, half + par)
                        if i == 3 and not last:
                            split_down(e + 1, 1 - par, half + par)
                        ga, gb = up_banks(i)
                        if bias is None:
                            ins = nc.scalar.activation(k.gate[0:M, i % 2, :], ga[0:M, :], ACTF)
                        else:
                            ins = nc.scalar.activation(k.gate[0:M, i % 2, :], gb[0:M, :], ACTF,
                                                       bias=bi[0:M, par, MT + m:MT + m + 1])
                        ins.then_inc(s_full, 1)
                        if i or not first:
                            high(JOBS * e + i - 1, i + 1)
                pairs(act, expert)
                high(JOBS * E - 1, 1)

            @block.gpsimd
            def _(pool):
                def low(n, out, whole, high):
                    pool.wait_ge(w_high, n + 1)
                    pool.sem_inc(passed, 1)
                    nc.gpsimd.tensor_tensor(out, whole, high.bitcast(F32), ALU.subtract).then_inc(w_low, 1)

                with pool.Fori(0, E // 2) as j:
                    for par in range(2):
                        low(4 * j + 2 * par, wL[par], wUp[:, par, :], wH[par])
                        low(4 * j + 2 * par + 1, dL[par], wD[0:M, par, :], dH[par])

            @block.vector
            def _(dve):
                dve.sem_inc(up_free, 2)
                dve.sem_inc(a_free, 2)
                nc.vector.memset(k.zero[:, :], 0.0).then_inc(seeded, 1)

                def low(n, i):
                    dve.wait_ge(f_high, n + 1)
                    nc.vector.tensor_tensor(fL[0:M, i % 2, :], k.hid[0:M, i % 2, :], fH[0:M, i % 2, :].bitcast(F32),
                                            ALU.subtract).then_inc(a_full, 1)

                for ch in range(NC):
                    cols = slice(ch * 512, (ch + 1) * 512)
                    dve.wait_ge(h_high, ch + 1)
                    nc.vector.tensor_tensor(hL[:, cols], hT[:, cols], hH[:, cols].bitcast(F32), ALU.subtract)\
                        .then_inc(h_low, 1)

                def expert(e, par, half, first=False, last=False):
                    dve.wait_ge(ld[par], NLD * (half + 1))
                    for i in range(JOBS):
                        ch, m = divmod(i, MT)
                        n = JOBS * e + i
                        dve.wait_ge(s_full, n + 1)
                        ga, gb = up_banks(i)
                        gate = k.gate[0:M, i % 2, :]
                        mul = k.gmul[0:M, i % 2, :]
                        if bias is None:
                            nc.vector.tensor_tensor(mul, gb[0:M, :], gate, ALU.mult).then_inc(up_free, 1)
                        else:
                            nc.vector.scalar_tensor_tensor(out=mul, in0=ga[0:M, :], scalar=bi[0:M, par, m:m + 1],
                                                           in1=gate, op0=ALU.add, op1=ALU.mult).then_inc(up_free, 1)
                        if i or not first:
                            low(n - 1, i + 1)
                        dve.wait_ge(up_free, n + 3)
                        nc.vector.tensor_tensor(k.hid[0:M, i % 2, :], mul, k.cb[0:M, par, ch * 512:(ch + 1) * 512],
                                                ALU.mult).then_inc(f_full, 1)

                pairs(dve, expert)
                low(JOBS * E - 1, 1)
                dve.wait_ge(y_full, 1)
                finish(dve, acc, chain)


def stage_linear(nc, k, hT, y):
    with ExitStack() as c:
        sem = lambda n: c.enter_context(nc.semaphore("lin" + n))
        sb = lambda n, s, d=F32: c.enter_context(nc.sbuf_tensor("lin" + n, s, d))
        ones, proj, taken, decayed, kv_full, kv_ready, q_turned, qT_ready = (
            sem(n) for n in ("ones", "proj", "taken", "decayed", "kv_full", "kv_ready", "q_turned", "qT_ready"))
        out_full, den_done, o_copied, rec_done, o_ready, o_turned, oT_ready, y_full = (
            sem(n) for n in ("out_full", "den_done", "o_copied", "rec_done", "o_ready", "o_turned", "oT_ready",
                             "y_full"))
        qkv = k.V2
        KV = sb("KV", [P, B, D + NH])
        qT = k.oU_flat
        oT = k.rB_flat
        den = sb("den", [P, NT, NH])
        rden = sb("rden", [P, NT, NH])
        o = k.tmp0
        with nc.Block() as block:
            @block.tensor
            def _(pe):
                pe.wait_ge(ones, 1)
                for t in range(NT + 2):
                    if t < NT:
                        if t >= 2:
                            pe.wait_ge(taken, t - 1)
                        nc.tensor.matmul(k.bank(t % 2)[:, 0:3 * D], hT[:, t * P:(t + 1) * P], k.lin_w[:, :],
                                         start=True, stop=True).then_inc(proj, 1)
                    if t >= 2:
                        u = t - 2
                        pe.wait_ge(decayed, u + 1)
                        ins = nc.tensor.matmul(k.bank(2 + u // TPB)[:, 0:D + 1], qkv[:, u, D:2 * D],
                                               qkv[:, u, 2 * D:3 * D + 1], start=(u % TPB == 0),
                                               stop=(u % TPB == TPB - 1))
                        if u % TPB == TPB - 1:
                            ins.then_inc(kv_full, 1)
                        ins = nc.tensor.transpose(k.bank(4 + u // 4)[:, (u % 4) * P:(u % 4 + 1) * P], qkv[:, u, 0:D],
                                                  k.ident[:, :])
                        if u % 4 == 3:
                            ins.then_inc(q_turned, 1)
                pe.wait_ge(kv_ready, B)
                for t in range(NT):
                    if t % 4 == 0:
                        pe.wait_ge(qT_ready, t // 4 + 1)
                    if t >= 4:
                        pe.wait_ge(o_copied, t - 3)
                    nc.tensor.matmul(k.bank(t % 4)[:, 0:D + NH], qT[:, t * P:(t + 1) * P], KV[:, t // TPB, :],
                                     start=True, stop=True).then_inc(out_full, 1)
                for t in range(NT):
                    if t % TPB == 0:
                        pe.wait_ge(o_ready, t // TPB + 1)
                    ins = nc.tensor.transpose(k.bank(4 + t // 4)[:, (t % 4) * P:(t % 4 + 1) * P], o[:, t, :],
                                              k.ident[:, :])
                    if t % 4 == 3:
                        ins.then_inc(o_turned, 1)
                for ch in range(NC):
                    pe.wait_ge(oT_ready, ch + 1)
                    nc.tensor.matmul(k.bank(ch), k.lin_wo[:, :], oT[:, ch * 512:(ch + 1) * 512],
                                     start=True, stop=True).then_inc(y_full, 1)

            @block.scalar
            def _(act):
                for t in range(NT):
                    act.wait_ge(taken, t + 1)
                    nc.scalar.activation(qkv[:, t, 0:2 * D], qkv[:, t, 0:2 * D], ACT.Relu,
                                         scale=k.dec[:, t % TPB:t % TPB + 1]).then_inc(decayed, 1)
                for ch in range(NC):
                    act.wait_ge(q_turned, ch + 1)
                    nc.scalar.copy(qT[:, ch * 512:(ch + 1) * 512], k.bank(4 + ch)).then_inc(qT_ready, 1)
                for t in range(NT):
                    act.wait_ge(den_done, t + 1)
                    nc.scalar.copy(o[:, t, :], k.bank(t % 4)[:, 0:D]).then_inc(o_copied, 1)
                for ch in range(NC):
                    act.wait_ge(o_turned, ch + 1)
                    nc.scalar.copy(oT[:, ch * 512:(ch + 1) * 512], k.bank(4 + ch)).then_inc(oT_ready, 1)

            @block.vector
            def _(dve):
                nc.vector.memset(qkv[:, :, 3 * D:3 * D + 1], 1.0).then_inc(ones, 1)
                for t in range(NT):
                    dve.wait_ge(proj, t + 1)
                    nc.vector.tensor_tensor(qkv[:, t, 0:3 * D], k.bank(t % 2)[:, 0:3 * D], k.row("lin_b"),
                                            ALU.add).then_inc(taken, 1)
                for b in range(B):
                    dve.wait_ge(kv_full, b + 1)
                    nc.vector.tensor_tensor(KV[:, b, 0:D], k.bank(2 + b)[:, 0:D], k.headmask[:, :], ALU.mult)
                    nc.vector.tensor_scalar(KV[:, b, D:D + NH], k.headsel[:, :], k.bank(2 + b)[:, D:D + 1], None,
                                            ALU.mult).then_inc(kv_ready, 1)
                for b in range(B):
                    for t in range(b * TPB, (b + 1) * TPB):
                        dve.wait_ge(out_full, t + 1)
                        nc.vector.tensor_scalar(den[:, t, :], k.bank(t % 4)[:, D:D + NH], RMS_EPS, None, ALU.add)\
                            .then_inc(den_done, 1)
                    tiles = slice(b * TPB, (b + 1) * TPB)
                    dve.wait_ge(den_done, (b + 1) * TPB)
                    nc.vector.reciprocal(rden[:, tiles, :], den[:, tiles, :]).then_inc(rec_done, 1)
                    dve.wait_ge(rec_done, b + 1)
                    dve.wait_ge(o_copied, (b + 1) * TPB)
                    ov = o[:, tiles, :].rearrange("p t (h e) -> p (t h) e", h=NH)
                    r = rden[:, tiles, :].rearrange("p t h -> p (t h)")
                    nc.vector.tensor_tensor(ov, ov, column(r, TPB * NH, D // NH), ALU.mult).then_inc(o_ready, 1)
                for ch in range(NC):
                    dve.wait_ge(y_full, ch + 1)
                    nc.vector.tensor_scalar(y[:, ch * 512:(ch + 1) * 512], k.bank(ch), k.col("lin_bo"),
                                            k.mod_col(1, 2, ch // CPB), ALU.add, ALU.mult)


def stage_rope(nc, k, qkv, q_dram, k_dram):
    HQK = NH + NKV
    hd = D // NH
    with ExitStack() as c:
        sem = lambda n: c.enter_context(nc.semaphore("rope" + n))
        sb = lambda n, s, d=F32: c.enter_context(nc.sbuf_tensor("rope" + n, s, d))
        chain, var_ready, std_ready, ready, turned, high, low, stored, cleared = (
            sem(n) for n in ("chain", "var", "std", "ready", "turned", "high", "low", "stored", "cleared"))
        r = k.rope_out
        sq = k.rope_sq
        ms = sb("ms", [P, 3, NT * HQK])
        qh = k.qA[1][:, :, :].rearrange("p h q -> p (h q)")
        kh = k.qB[0][0:32, :, :].rearrange("p h q -> p (h q)")
        with nc.Block() as block:
            @block.vector
            def _(dve):
                n = [0]

                def link(ins):
                    n[0] += 1
                    ins.then_inc(chain, 1)
                    dve.wait_ge(chain, n[0])

                for b in range(B):
                    tiles = slice(b * TPB, (b + 1) * TPB)
                    x = qkv[:, tiles, 0:HQK * hd].rearrange("p t (h e) -> p t h e", h=HQK)
                    o = r[:, tiles, :].rearrange("p t (h e) -> p t h e", h=HQK)
                    s = sq[:, tiles, :].rearrange("p t (h e) -> p t h e", h=HQK)
                    cos, sin = (k.rope[:, i, :, :].unsqueeze(2).broadcast_to((P, TPB, HQK, hd // 2)) for i in range(2))
                    lo, hi = slice(0, hd // 2), slice(hd // 2, hd)
                    link(nc.vector.tensor_tensor(o[:, :, :, lo], x[:, :, :, lo], cos, ALU.mult))
                    link(nc.vector.tensor_tensor(o[:, :, :, hi], x[:, :, :, lo], sin, ALU.mult))
                    link(nc.vector.tensor_tensor(s[:, :, :, lo], x[:, :, :, hi], sin, ALU.mult))
                    link(nc.vector.tensor_tensor(s[:, :, :, hi], x[:, :, :, hi], cos, ALU.mult))
                    link(nc.vector.tensor_tensor(o[:, :, :, lo], o[:, :, :, lo], s[:, :, :, lo], ALU.subtract))
                    link(nc.vector.tensor_tensor(o[:, :, :, hi], o[:, :, :, hi], s[:, :, :, hi], ALU.add))
                link(nc.vector.tensor_copy(k.V[:, :, 0:NKV * hd], qkv[:, :, HQK * hd:]))
                link(nc.vector.tensor_tensor(sq[:, :, :], r[:, :, :], r[:, :, :], ALU.mult))
                rv = r[:, :, :].rearrange("p t (h e) -> p (t h) e", h=HQK)
                link(nc.vector.tensor_reduce(ms[:, 0, :], sq[:, :, :].rearrange("p t (h e) -> p (t h) e", h=HQK), AX,
                                             ALU.add))
                nc.vector.tensor_scalar(ms[:, 0, :], ms[:, 0, :], 1.0 / hd, RMS_EPS, ALU.mult, ALU.add)\
                    .then_inc(var_ready, 1)
                dve.wait_ge(std_ready, 1)
                link(nc.vector.reciprocal(ms[:, 2, :], ms[:, 1, :]))
                link(nc.vector.tensor_tensor(rv, rv, column(ms[:, 2, :], NT * HQK, hd), ALU.mult))
                w = k.row("qk_w").unsqueeze(1).broadcast_to((P, NT, HQK * hd))
                nc.vector.tensor_tensor(r[:, :, :], r[:, :, :], w, ALU.mult).then_inc(ready, 1)
                for ch in range(NC):
                    cols = slice(ch * 512, (ch + 1) * 512)
                    lows = slice(T + ch * 512, T + (ch + 1) * 512)
                    dve.wait_ge(high, 2 * ch + 2)
                    nc.vector.tensor_tensor(qh[:, lows], k.bank(ch), qh[:, cols].bitcast(F32), ALU.subtract)\
                        .then_inc(low, 1)
                    nc.vector.tensor_tensor(kh[:, lows], k.bank(4 + ch)[0:32, :], kh[:, cols].bitcast(F32),
                                            ALU.subtract).then_inc(low, 1)

            @block.scalar
            def _(act):
                act.wait_ge(var_ready, 1)
                nc.scalar.activation(ms[:, 1, :], ms[:, 0, :], ACT.Sqrt).then_inc(std_ready, 1)
                for ch in range(NC):
                    cols = slice(ch * 512, (ch + 1) * 512)
                    act.wait_ge(turned, ch + 1)
                    nc.scalar.copy(qh[:, cols], k.bank(ch)).then_inc(high, 1)
                    nc.scalar.copy(kh[:, cols], k.bank(4 + ch)[0:32, :]).then_inc(high, 1)

            @block.tensor
            def _(pe):
                pe.wait_ge(ready, 1)
                for t in range(NT):
                    cols = slice((t % 4) * P, (t % 4 + 1) * P)
                    nc.tensor.transpose(k.bank(t // 4)[:, cols], r[:, t, 0:D], k.ident[:, :])
                    ins = nc.tensor.transpose(k.bank(4 + t // 4)[0:32, cols], r[:, t, D:D + 32], k.ident[:, :])
                    if t % 4 == 3:
                        ins.then_inc(turned, 1)

            @block.gpsimd
            def _(pool):
                nc.gpsimd.memset(k.qA[0][:, :, :].bitcast(F32), 0.0)
                for stack in (k.kL[0], k.kL[1], k.kH[0], k.kH[1]):
                    ins = nc.gpsimd.memset(stack[:, :].bitcast(F32), 0.0)
                ins.then_inc(cleared, 1)
                pool.wait_ge(cleared, 1)
                for p in range(2):
                    nc.gpsimd.memset(k.kH[p][4 * hd:4 * hd + 1, :].bitcast(F32), 1.0)

            @block.sync
            def _(sp):
                sp.wait_ge(low, 2 * NC)
                for part in range(2):
                    cols = slice(part * T, (part + 1) * T)
                    sp.dma_start(q_dram[part].rearrange("h d q -> (h d) q"), qh[:, cols].bitcast(F32)).then_inc(stored, 16)
                    for copy in range(2):
                        at = (2 * part + copy) * hd
                        sp.dma_start(k_dram[:, at:at + hd, :].rearrange("h d q -> h d q"),
                                     kh[:, cols].bitcast(F32)).then_inc(stored, 16)
                sp.wait_ge(stored, 96)


def stage_gate(nc, k, hT, oT):
    g = k.tmp1_flat
    with ExitStack() as c:
        sem = lambda n: c.enter_context(nc.semaphore("gate" + n))
        gate_full, gated, prod, out_full = (sem(n) for n in ("full", "gated", "prod", "out"))
        with nc.Block() as block:
            @block.tensor
            def _(pe):
                for ch in range(NC):
                    nc.tensor.matmul(k.bank(ch), k.wg[:, :], oT[:, ch * 512:(ch + 1) * 512], start=True,
                                     stop=True).then_inc(gate_full, 1)
                for ch in range(NC):
                    pe.wait_ge(prod, ch + 1)
                    nc.tensor.matmul(k.bank(4 + ch), k.wo1[:, :], oT[:, ch * 512:(ch + 1) * 512], start=True,
                                     stop=True).then_inc(out_full, 1)

            @block.scalar
            def _(act):
                for ch in range(NC):
                    act.wait_ge(gate_full, ch + 1)
                    nc.scalar.activation(g[:, ch * 512:(ch + 1) * 512], k.bank(ch), ACT.Sigmoid,
                                         bias=k.col("bg")).then_inc(gated, 1)

            @block.vector
            def _(dve):
                for ch in range(NC):
                    cols = slice(ch * 512, (ch + 1) * 512)
                    dve.wait_ge(gated, ch + 1)
                    nc.vector.tensor_tensor(oT[:, cols], oT[:, cols], g[:, cols], ALU.mult).then_inc(prod, 1)
                for ch in range(NC):
                    cols = slice(ch * 512, (ch + 1) * 512)
                    dve.wait_ge(out_full, ch + 1)
                    nc.vector.scalar_tensor_tensor(out=hT[:, cols], in0=k.bank(4 + ch), scalar=k.col("ffn_bo"),
                                                   in1=hT[:, cols], op0=ALU.add, op1=ALU.add)


def stage_store(nc, k, out):
    with ExitStack() as c:
        stored = c.enter_context(nc.semaphore("out_stored"))
        with nc.Block() as block:
            @block.sync
            def _(sp):
                sp.dma_start(out.rearrange("b (t p) d -> p (b t) d", p=P), k.x[:, :, :]).then_inc(stored, 16)
                sp.wait_ge(stored, 16)


COLS = ["lin_bo", "bg", "ffn_bo", "ln1", "ln2"]
ROWS = [("e_bias", 32), ("lin_b", 3 * D), ("ffn_b", 192), ("qk_w", 160), ("br", 8)]


def program(nc, a, out):
    k = Core()
    with ExitStack() as c:
        sb = lambda n, s, d=F32: c.enter_context(nc.sbuf_tensor(n, s, d))
        k.ps = c.enter_context(nc.psum_tensor("ps", [P, 8 * 512], F32))
        k.bank = lambda i: k.ps[:, i * 512:(i + 1) * 512]
        k.x = sb("x_res", [P, NT, D])
        k.hT = sb("hT", [P, T])
        k.y = sb("y", [P, T])
        k.cT = k.y
        k.qA = [sb(f"qA{p}", [P, REP, S], F32R) for p in range(2)]
        k.qB = [sb(f"qB{p}", [65, REP, S], F32R) for p in range(2)]
        k.kH = [sb(f"kH{p}", [P, S], F32R) for p in range(2)]
        k.kL = [sb(f"kL{p}", [P, S], F32R) for p in range(2)]
        k.Vg = [sb(f"Vg{p}", [P, TPB, 65]) for p in range(2)]
        k.oU = sb("oU", [P, REP, S])
        k.rB = sb("rB", [P, REP * S])
        shared = sb("shared", [P, 8 * S])
        k.V = shared[:, 0:4 * S].rearrange("p (t n) -> p t n", t=NT)
        PTf = shared[:, 4 * S:6 * S]
        k.PT = PTf.rearrange("p (s q) -> p s q", s=2)
        k.oN = shared[:, 6 * S:8 * S].rearrange("p (c q) -> p c q", c=2)
        k.PT8 = shared[:, :].rearrange("p (s q) -> p s q", s=8)
        k.oU8, k.oN8 = k.oU[:, 0, :], k.oU[:, 1, :]
        V1 = k.rB[:, 3 * S:3 * S + NT * 32].rearrange("p (t n) -> p t n", t=NT)
        k.cb = shared[:, 0:4 * S].rearrange("p (s q) -> p s q", s=2)
        k.gate = PTf[:, 0:S].rearrange("p (s q) -> p s q", s=2)
        k.gmul = PTf[:, S:2 * S].rearrange("p (s q) -> p s q", s=2)
        k.hid = shared[:, 6 * S:7 * S].rearrange("p (s q) -> p s q", s=2)
        k.V2 = shared[:, 0:NT * (3 * D + 1)].rearrange("p (t n) -> p t n", t=NT)
        ffn_qkv = shared[:, 0:NT * 192].rearrange("p (t n) -> p t n", t=NT)
        oUf = k.oU[:, :, :].rearrange("p h q -> p (h q)")
        k.oU_flat = oUf[:, 0:T]
        k.rB_flat = k.rB[:, 0:T]
        k.tmp0_flat = oUf[:, T:2 * T]
        k.tmp0 = k.tmp0_flat.rearrange("p (t d) -> p t d", t=NT)
        k.tmp1_flat = k.rB[:, T:2 * T]
        k.tmp1 = k.tmp1_flat.rearrange("p (t d) -> p t d", t=NT)
        k.rope_out = oUf[:, 0:NT * 160].rearrange("p (t n) -> p t n", t=NT)
        k.rope_sq = k.rB[:, 0:NT * 160].rearrange("p (t n) -> p t n", t=NT)
        k.wqk = sb("wqk", [P, 2, 3 * P])
        k.woG = sb("woG", [P, 2, D])
        k.mraw = sb("mraw", [P, 2, REP * TPB])
        k.mmax = sb("mmax", [P, REP * TPB])
        k.mT = sb("mT", [16, 2, P], F32R)
        k.sm = sb("sm", [P, REP * S // P])
        k.rs = sb("rs", [P, REP * S // P])
        k.ident = sb("ident", [P, P])
        k.ident_bf = sb("ident_bf", [P, P], BF16)
        k.masks = sb("masks", [P, 2, P], BF16)
        k.mod = sb("mod", [P, 2, 6, B])
        k.dec = sb("dec", [P, TPB])
        k.rope = sb("rope", [P, 2, TPB, 4])
        k.iota = sb("iota", [P, 32])
        k.headmask = sb("headmask", [P, D])
        k.headsel = sb("headsel", [P, NH])
        k.cols = sb("cols", [P, len(COLS)])
        k.rows = sb("rows", [P, sum(n for _, n in ROWS)])
        k.one_col = sb("one_col", [P, 1])
        k.zero = sb("zero", [1, P])
        k.wv0 = sb("wv0", [P, 256])
        k.gate0 = sb("gate0", [P, 32])
        k.lin_w = sb("lin_w", [P, 3 * D])
        k.lin_wo = sb("lin_wo", [P, D])
        k.ffn_w = sb("ffn_w", [P, 192])
        k.wg = sb("wg", [P, D])
        k.wo1 = sb("wo1", [P, D])
        k.wr = sb("wr", [P, 8])
        k.b2 = sb("b2", [8, D])
        k.logits = sb("logits", [P, NT, 32])
        starts = {}
        at = 0
        for nme, w in ROWS:
            starts[nme] = (at, w)
            at += w
        k.row = lambda nme: k.rows[:, starts[nme][0]:starts[nme][0] + starts[nme][1]]
        k.col = lambda nme: k.cols[:, COLS.index(nme):COLS.index(nme) + 1]
        k.mod_col = lambda layer, j, b: k.mod[:, layer, j, b:b + 1]
        dram = lambda n, s: nc.dram_tensor(n, s, F32, kind="Internal").ap()
        comb0, comb1 = dram("comb0", (32, T)), dram("comb1", (8, T))
        q_dram, k_dram = dram("q_split", (2, NH, 8, T)), dram("k_split", (NKV, 32, T))
        o_dram = dram("o_heads", (NH, 8, T))

        k.norm_sems = [c.enter_context(nc.semaphore("norm_" + n)) for n in (
            "xc", "sq", "var", "std", "xn", "turned", "out_act", "out_dve", "tile", "stored")]
        k.turn_sem = c.enter_context(nc.semaphore("turn_turned"))
        k.norm_uses = k.norm_centred = k.norm_tiles = k.turn_uses = 0

        k.params_ld = c.enter_context(nc.semaphore("params_ld"))
        stage_load(nc, k, a)

        m0 = lambda j: (lambda b: k.mod_col(0, j, b))
        m1 = lambda j: (lambda b: k.mod_col(1, j, b))

        def store_v(dve, t, bank):
            return nc.vector.tensor_copy(k.V[:, t, :], bank)

        stage_norm(nc, k, "n0", k.x, k.hT, True, LN_EPS, m0(1), m0(0), (k.wv0[:, :], 256, store_v))
        with nc.Block() as block:
            @block.gpsimd
            def _(pool):
                nc.gpsimd.memset(k.y[:, :], 0.0)

            @block.sync
            def _(sp):
                sp.wait_ge(k.params_ld, 16 * k.n_params)
        stage_attention64(nc, k, "a0", k.hT, a["wqk0"], a["wo0"], k.y)

        def scale_y(layer, j):
            def pre(dve, ch):
                yc = k.y[:, ch * 512:(ch + 1) * 512]
                return nc.vector.tensor_scalar(yc, yc, k.mod_col(layer, j, ch // CPB), None, ALU.mult)
            return pre

        stage_turn(nc, k, "t0", k.y, k.x, True, scale_y(0, 2))

        def store_logits(E, bias):
            def store(dve, t, bank):
                o = k.logits[:, t, 0:E]
                if bias is None:
                    return nc.vector.tensor_copy(o, bank)
                return nc.vector.tensor_tensor(o, bank, bias, ALU.add)
            return store

        stage_norm(nc, k, "n1", k.x, k.hT, True, LN_EPS, m0(4), m0(3), (k.gate0[:, :], 32, store_logits(32, None)))
        stage_combine(nc, k, "c0", 32, k.logits, comb0, True, k.row("e_bias"))

        def finish0(dve, acc, chain):
            for ch in range(NC):
                nc.vector.tensor_scalar(k.y[:, ch * 512:(ch + 1) * 512], acc(ch), k.mod_col(0, 5, ch // CPB), None,
                                        ALU.mult)

        stage_experts(nc, k, "e0", 32, 96, 1, k.hT, a["w1"], a["w3"], a["w2"], None, comb0, None, finish0)
        stage_turn(nc, k, "t1", k.y, k.x, True)

        stage_norm(nc, k, "n2", k.x, k.hT, True, LN_EPS, m1(1), m1(0))
        stage_linear(nc, k, k.hT, k.y)
        stage_turn(nc, k, "t2", k.y, k.x, True)

        stage_norm(nc, k, "n3", k.x, k.hT, True, LN_EPS, m1(4), m1(3))
        h_tok = k.tmp0
        h1T = k.y
        stage_turn(nc, k, "t3", k.hT, h_tok, False)

        def store_qkv(dve, t, bank):
            return nc.vector.tensor_tensor(ffn_qkv[:, t, :], bank, k.row("ffn_b"), ALU.add)

        stage_norm(nc, k, "n4", h_tok, h1T, False, RMS_EPS, lambda b: k.col("ln1"), None,
                   (k.ffn_w[:, :], 192, store_qkv))
        k.V = V1
        stage_rope(nc, k, ffn_qkv, q_dram, k_dram)
        stage_attention8(nc, k, "a1", q_dram, k_dram, o_dram, k.tmp0_flat)
        stage_gate(nc, k, k.hT, k.tmp0_flat)
        stage_turn(nc, k, "t4", k.hT, h_tok, False)
        h2T = k.rB_flat
        stage_norm(nc, k, "n5", h_tok, h2T, False, RMS_EPS, lambda b: k.col("ln2"), None,
                   (k.wr[:, :], 8, store_logits(8, k.row("br"))))
        stage_combine(nc, k, "c1", 8, k.logits[:, :, 0:8], comb1, False, None)

        def finish1(dve, acc, chain):
            for ch in range(NC):
                yc = k.y[:, ch * 512:(ch + 1) * 512]
                nc.vector.tensor_tensor(yc, acc(ch), k.hT[:, ch * 512:(ch + 1) * 512], ALU.add).then_inc(chain, 1)
                dve.wait_ge(chain, ch + 1)
                nc.vector.tensor_scalar(yc, yc, k.mod_col(1, 5, ch // CPB), None, ALU.mult)

        stage_experts(nc, k, "e1", 8, P, 2, h2T, a["W1a"], a["W1b"], a["W2"], a["b1"], comb1, k.b2, finish1)
        stage_turn(nc, k, "t5", k.y, k.x, True)
        stage_store(nc, k, out)


def constants():
    f = np.float32
    i = np.arange(P)
    hd = D // NH
    masks = np.zeros((P, 2, P), f)
    masks[:, 0, :] = np.where(i[:, None] > i[None, :], MASKED, 0.0)
    masks[:, 1, :] = np.where(i[None, :] > i[:, None], MASKED, 0.0)
    pos = np.arange(S, dtype=f)
    dec = np.exp(-pos / f(S)).astype(f).reshape(TPB, P).T
    inv = (1.0 / f(10000.0) ** (np.arange(0, hd, 2, dtype=f) / f(hd))).astype(f)
    ang = (pos[:, None] * inv[None, :]).astype(f)
    rope = np.stack([np.cos(ang), np.sin(ang)]).astype(f).reshape(2, TPB, P, hd // 2).transpose(2, 0, 1, 3)
    head = i // hd
    return {
        "ident": np.eye(P, dtype=f), "masks": masks, "dec": dec, "rope": rope,
        "iota": np.tile(np.arange(32, dtype=f), (P, 1)),
        "headmask": (head[:, None] == head[None, :]).astype(f),
        "headsel": (head[:, None] == np.arange(NH)[None, :]).astype(f),
    }


def layout(inp):
    g = {n: np.asarray(v) for n, v in inp.items()}
    t = lambda n: g[n].T
    cols = {"lin_bo": g["L1_attn_b_o"], "bg": np.tile(g["L1_ffn_bg"], NH), "ffn_bo": g["L1_ffn_bo"],
            "ln1": g["L1_ffn_ln1_w"], "ln2": g["L1_ffn_ln2_w"]}
    rows = {"e_bias": g["L0_ffn_e_bias"],
            "lin_b": np.concatenate([g["L1_attn_b_q"], g["L1_attn_b_k"], g["L1_attn_b_v"]]),
            "ffn_b": np.concatenate([g["L1_ffn_bq"], g["L1_ffn_bk"], g["L1_ffn_bv"]]),
            "qk_w": np.concatenate([np.tile(g["L1_ffn_qn_w"], NH), np.tile(g["L1_ffn_kn_w"], NKV)]),
            "br": g["L1_ffn_br"]}
    wq = t("L0_attn_Wq").reshape(D, NKV, 2 * P)
    wk = t("L0_attn_Wk").reshape(D, NKV, 64)
    wqk = np.concatenate([wk, wk, wq], axis=2).transpose(1, 0, 2)
    wo0 = t("L0_attn_Wo").reshape(NKV, 2, P, D).transpose(0, 2, 1, 3)
    wg = np.zeros((P, P), g["L1_ffn_Wg"].dtype)
    for h in range(NH):
        wg[8 * h:8 * h + 8, 8 * h:8 * h + 8] = g["L1_ffn_Wg"]
    W1 = g["L1_ffn_W1"]
    return {
        "x": g["L0_attn_hidden_states"],
        "cT": np.stack([t("L0_c"), t("L1_c")], axis=1),
        "wmod": np.stack([g["L0_wmod"], g["L1_wmod"]], axis=1),
        "cols": np.stack([cols[n] for n in COLS], axis=1),
        "rows": np.concatenate([rows[n] for n, _ in ROWS])[None, :],
        "wv0": t("L0_attn_Wv"), "gate0": t("L0_ffn_gate_w"),
        "lin_w": np.concatenate([t("L1_attn_W_q"), t("L1_attn_W_k"), t("L1_attn_W_v")], axis=1),
        "lin_wo": t("L1_attn_W_o"),
        "ffn_w": np.concatenate([g["L1_ffn_Wq"], g["L1_ffn_Wk"], g["L1_ffn_Wv"]], axis=1),
        "wg": wg, "wo1": g["L1_ffn_Wo"], "wr": g["L1_ffn_Wr"], "b2": g["L1_ffn_b2"],
        "wqk0": wqk, "wo0": wo0,
        "w1": g["L0_ffn_w1"], "w3": g["L0_ffn_w3"], "w2": g["L0_ffn_w2"],
        "W1a": W1[:, :, 0:256], "W1b": W1[:, :, 256:512],
        "W2": g["L1_ffn_W2"].reshape(8, 2, P, D).transpose(0, 2, 1, 3).reshape(8, P, 2 * D),
        "b1": g["L1_ffn_b1"].reshape(8, 4, P).transpose(0, 2, 1),
    }


def kernel(**inputs):
    import concourse.bacc as bacc
    from concourse.bass_utils import run_bass_kernel_spmd as run

    nc = bacc.Bacc("TRN2", target_bir_lowering=False, num_devices=1)
    arrays = {n: np.ascontiguousarray(v) for n, v in {**layout(inputs), **constants()}.items()}
    a = {n: nc.dram_tensor("in_" + n, v.shape, mybir.dt.from_np(v.dtype), kind="ExternalInput").ap()
         for n, v in arrays.items()}
    out = nc.dram_tensor("out", arrays["x"].shape, F32, kind="ExternalOutput").ap()
    program(nc, a, out)
    r = run(nc, [{"in_" + n: v for n, v in arrays.items()}], core_ids=[0])
    return r.results[0]["out"]
```
